# Optimizing a Trainium2 kernel written in Bass

```python
import numpy as np
import jax
import jax.numpy as jnp

def _softmax(x, axis=-1):
    return jax.nn.softmax(x, axis=axis)

def _gelu(x):
    return jax.nn.gelu(x, approximate=True)

def _silu(x):
    return jax.nn.silu(x)

def _sigmoid(x):
    return jax.nn.sigmoid(x)

def _layernorm(x, axis=-1, eps=1e-05):
    m = jnp.mean(x, axis=axis, keepdims=True)
    v = jnp.var(x, axis=axis, keepdims=True)
    return (x - m) / jnp.sqrt(v + eps)

def _scatter_add(tgt, idx, src, axis=0):
    return tgt.at[idx].add(src)

def _segment_sum(src, seg, n):
    return jax.ops.segment_sum(src, seg, n)
kernel_name = 'mk_cond_seq_d2_seqx_r8_d9d811'

def setup_inputs(seed: int=0):
    np.random.seed(seed)
    _w = jnp.asarray

    def _rec_inputs():
        import jax
        import jax.numpy as jnp
        _rk = jax.random.key(seed)
        x = 7.22e-05 + 1 * jax.random.normal(jax.random.fold_in(_rk, 1), (32, 32, 128), jnp.float32)
        _lenS = 32 - jax.random.randint(jax.random.fold_in(_rk, 7), (32,), 0, max(1, 32 // 4) + 1, jnp.int32)
        _lenS2 = 32 - jax.random.randint(jax.random.fold_in(_rk, 8), (32,), 0, max(1, 32 // 4) + 1, jnp.int32)
        cond_1024 = 0.00782532 + 1.00527 * jax.random.normal(jax.random.fold_in(_rk, 11), (32, 128), jnp.float32)
        return (x, cond_1024)
    x, cond_1024 = _rec_inputs()

    def _L0_cond_setup():
        import jax, jax.numpy as jnp
        import numpy as np
        EPS = 1e-06

        def _ln(x):
            m = jnp.mean(x, axis=-1, keepdims=True)
            v = jnp.mean(jnp.square(x - m), axis=-1, keepdims=True)
            return (x - m) * jax.lax.rsqrt(v + EPS)

        def _modulate(x, shift, scale):
            return x * (1.0 + scale[:, None]) + shift[:, None]
        key = jax.random.key(seed)
        B, S, H, NH = (8, 128, 128, 16)
        ks = jax.random.split(key, 12)
        s = lambda k, sh: jax.random.normal(k, sh, dtype=jnp.float32) * 0.02
        return {'x': jax.random.normal(ks[0], (B, S, H), dtype=jnp.float32), 'c': jax.random.normal(ks[1], (B, H), dtype=jnp.float32), 'w_ada': s(ks[2], (H, 6 * H)), 'b_ada': jnp.zeros((6 * H,), dtype=jnp.float32), 'w_qkv': s(ks[3], (H, 3 * H)), 'w_proj': s(ks[4], (H, H)), 'b_proj': jnp.zeros((H,), dtype=jnp.float32), 'w_mlp1': s(ks[5], (H, 4 * H)), 'b_mlp1': jnp.zeros((4 * H,), dtype=jnp.float32), 'w_mlp2': s(ks[6], (4 * H, H)), 'b_mlp2': jnp.zeros((H,), dtype=jnp.float32)}
    _L0_cond_all = _L0_cond_setup()
    _L0_cond_in = {k: v for k, v in _L0_cond_all.items() if k in ('w_ada', 'b_ada', 'w_qkv', 'w_proj', 'b_proj', 'w_mlp1', 'b_mlp1', 'w_mlp2', 'b_mlp2')}
    del _L0_cond_all

    def _L1_cond_setup():
        import jax, jax.numpy as jnp
        import numpy as np
        D = 128
        H = 16
        DH = D // H
        FF = int(D * 2.0)
        EPS = 1e-06

        def _ln(t):
            mu = jnp.mean(t, axis=-1, keepdims=True)
            var = jnp.mean((t - mu) ** 2, axis=-1, keepdims=True)
            return (t - mu) * jax.lax.rsqrt(var + EPS)
        key = jax.random.key(seed)
        ks = jax.random.split(key, 16)
        B, L = (2, 256)
        s = 0.02
        return {'x': jax.random.normal(ks[0], (B, L, D), jnp.float32), 'c': jax.random.normal(ks[1], (B, 1, D), jnp.float32), 'Wq': jax.random.normal(ks[2], (D, D), jnp.float32) * s, 'bq': jnp.zeros((D,), jnp.float32), 'Wk': jax.random.normal(ks[3], (D, D), jnp.float32) * s, 'bk': jnp.zeros((D,), jnp.float32), 'Wv': jax.random.normal(ks[4], (D, D), jnp.float32) * s, 'bv': jnp.zeros((D,), jnp.float32), 'Wo': jax.random.normal(ks[5], (D, D), jnp.float32) * s, 'bo': jnp.zeros((D,), jnp.float32), 'W1': jax.random.normal(ks[6], (D, FF), jnp.float32) * s, 'b1': jnp.zeros((FF,), jnp.float32), 'W2': jax.random.normal(ks[7], (FF, D), jnp.float32) * s, 'b2': jnp.zeros((D,), jnp.float32), 'Wada': jax.random.normal(ks[8], (D, 6 * D), jnp.float32) * s, 'bada': jnp.zeros((6 * D,), jnp.float32)}
    _L1_cond_all = _L1_cond_setup()
    _L1_cond_in = {k: v for k, v in _L1_cond_all.items() if k in ('Wq', 'bq', 'Wk', 'bk', 'Wv', 'bv', 'Wo', 'bo', 'W1', 'b1', 'W2', 'b2', 'Wada', 'bada')}
    del _L1_cond_all
    return {'x': x, 'cond_1024': cond_1024, 'L0_cond_w_ada': _L0_cond_in['w_ada'], 'L0_cond_b_ada': _L0_cond_in['b_ada'], 'L0_cond_w_qkv': _L0_cond_in['w_qkv'], 'L0_cond_w_proj': _L0_cond_in['w_proj'], 'L0_cond_b_proj': _L0_cond_in['b_proj'], 'L0_cond_w_mlp1': _L0_cond_in['w_mlp1'], 'L0_cond_b_mlp1': _L0_cond_in['b_mlp1'], 'L0_cond_w_mlp2': _L0_cond_in['w_mlp2'], 'L0_cond_b_mlp2': _L0_cond_in['b_mlp2'], 'L1_cond_Wq': _L1_cond_in['Wq'], 'L1_cond_bq': _L1_cond_in['bq'], 'L1_cond_Wk': _L1_cond_in['Wk'], 'L1_cond_bk': _L1_cond_in['bk'], 'L1_cond_Wv': _L1_cond_in['Wv'], 'L1_cond_bv': _L1_cond_in['bv'], 'L1_cond_Wo': _L1_cond_in['Wo'], 'L1_cond_bo': _L1_cond_in['bo'], 'L1_cond_W1': _L1_cond_in['W1'], 'L1_cond_b1': _L1_cond_in['b1'], 'L1_cond_W2': _L1_cond_in['W2'], 'L1_cond_b2': _L1_cond_in['b2'], 'L1_cond_Wada': _L1_cond_in['Wada'], 'L1_cond_bada': _L1_cond_in['bada']}

def reference(x, cond_1024, L0_cond_w_ada, L0_cond_b_ada, L0_cond_w_qkv, L0_cond_w_proj, L0_cond_b_proj, L0_cond_w_mlp1, L0_cond_b_mlp1, L0_cond_w_mlp2, L0_cond_b_mlp2, L1_cond_Wq, L1_cond_bq, L1_cond_Wk, L1_cond_bk, L1_cond_Wv, L1_cond_bv, L1_cond_Wo, L1_cond_bo, L1_cond_W1, L1_cond_b1, L1_cond_W2, L1_cond_b2, L1_cond_Wada, L1_cond_bada):
    import jax
    import jax.numpy as jnp

    def _L0_cond_ref(x, c, w_ada, b_ada, w_qkv, w_proj, b_proj, w_mlp1, b_mlp1, w_mlp2, b_mlp2):
        import jax, jax.numpy as jnp
        import numpy as np
        EPS = 1e-06

        def _ln(x):
            m = jnp.mean(x, axis=-1, keepdims=True)
            v = jnp.mean(jnp.square(x - m), axis=-1, keepdims=True)
            return (x - m) * jax.lax.rsqrt(v + EPS)

        def _modulate(x, shift, scale):
            return x * (1.0 + scale[:, None]) + shift[:, None]
        B, S, H = x.shape
        NH = 16
        CH = H // NH
        cmod = jax.nn.silu(c) @ w_ada + b_ada
        shift_msa, scale_msa, gate_msa, shift_mlp, scale_mlp, gate_mlp = jnp.split(cmod, 6, axis=-1)
        x_mod = _modulate(_ln(x), shift_msa, scale_msa)
        qkv = x_mod @ w_qkv
        k, q, v = jnp.split(qkv, 3, axis=-1)
        k = k.reshape(B, S, NH, CH)
        q = q.reshape(B, S, NH, CH)
        v = v.reshape(B, S, NH, CH)
        q = q / CH
        w = jnp.einsum('bqhc,bkhc->bhqk', q, k).astype(jnp.float32)
        w = jax.nn.softmax(w, axis=-1)
        y = jnp.einsum('bhqk,bkhc->bqhc', w, v).reshape(B, S, H)
        attn_x = y @ w_proj + b_proj
        x = x + gate_msa[:, None] * attn_x
        x_mod2 = _modulate(_ln(x), shift_mlp, scale_mlp)
        h = jax.nn.gelu(x_mod2 @ w_mlp1 + b_mlp1)
        mlp_x = h @ w_mlp2 + b_mlp2
        x = x + gate_mlp[:, None] * mlp_x
        return x

    def _L1_cond_ref(x, c, Wq, bq, Wk, bk, Wv, bv, Wo, bo, W1, b1, W2, b2, Wada, bada):
        import jax, jax.numpy as jnp
        import numpy as np
        D = 128
        H = 16
        DH = D // H
        FF = int(D * 2.0)
        EPS = 1e-06

        def _ln(t):
            mu = jnp.mean(t, axis=-1, keepdims=True)
            var = jnp.mean((t - mu) ** 2, axis=-1, keepdims=True)
            return (t - mu) * jax.lax.rsqrt(var + EPS)
        B, L, _ = x.shape
        ada = jax.nn.silu(c) @ Wada + bada
        shift_msa, scale_msa, gate_msa, shift_mlp, scale_mlp, gate_mlp = jnp.split(ada, 6, axis=-1)
        h = _ln(x) * (1.0 + scale_msa) + shift_msa
        q = (h @ Wq + bq).reshape(B, L, H, DH)
        k = (h @ Wk + bk).reshape(B, L, H, DH)
        v = (h @ Wv + bv).reshape(B, L, H, DH)
        scale = 1.0 / np.sqrt(DH).astype(np.float32)
        scores = jnp.einsum('blhe,bshe->bhls', q, k)
        A = jax.nn.softmax(scale * scores, axis=-1)
        out = jnp.einsum('bhls,bshd->blhd', A, v)
        out = jnp.transpose(out, (0, 2, 1, 3)).reshape(B, L, H * DH)
        x = x + gate_msa * (out @ Wo + bo)
        h2 = _ln(x) * (1.0 + scale_mlp) + shift_mlp
        m = jax.nn.gelu(h2 @ W1 + b1, approximate=False) @ W2 + b2
        return x + gate_mlp * m
    x = _L0_cond_ref(x, cond_1024, L0_cond_w_ada, L0_cond_b_ada, L0_cond_w_qkv, L0_cond_w_proj, L0_cond_b_proj, L0_cond_w_mlp1, L0_cond_b_mlp1, L0_cond_w_mlp2, L0_cond_b_mlp2)
    x = _L1_cond_ref(x, cond_1024[:, None, :], L1_cond_Wq, L1_cond_bq, L1_cond_Wk, L1_cond_bk, L1_cond_Wv, L1_cond_bv, L1_cond_Wo, L1_cond_bo, L1_cond_W1, L1_cond_b1, L1_cond_W2, L1_cond_b2, L1_cond_Wada, L1_cond_bada)
    return x

_drawn_inputs = setup_inputs


def setup_inputs(seed=0):
    import zlib

    import numpy as np

    out = dict(_drawn_inputs(seed))
    spreads = {'L0_cond_b_ada': (0.0, 0.528),
     'L0_cond_b_proj': (0.0, 0.465),
     'L0_cond_b_mlp1': (0.0, 0.8),
     'L0_cond_b_mlp2': (0.0, 0.507),
     'L1_cond_bq': (0.0, 0.8),
     'L1_cond_bk': (0.0, 0.8),
     'L1_cond_bv': (0.0, 0.8),
     'L1_cond_bo': (0.0, 0.494),
     'L1_cond_b1': (0.0, 0.8),
     'L1_cond_b2': (0.0, 0.502),
     'L1_cond_bada': (0.0, 0.566)}
    factors = {'L0_cond_w_ada': 2.855,
     'L0_cond_w_qkv': 8.0,
     'L0_cond_w_proj': 8.0,
     'L0_cond_w_mlp1': 6.05,
     'L0_cond_w_mlp2': 5.537,
     'L1_cond_Wq': 8.0,
     'L1_cond_Wk': 8.0,
     'L1_cond_Wv': 8.0,
     'L1_cond_Wo': 8.0,
     'L1_cond_W1': 8.0,
     'L1_cond_W2': 7.978,
     'L1_cond_Wada': 2.915}
    for name, (base, spread) in spreads.items():
        noise = np.random.default_rng([zlib.crc32(name.encode()), seed]).standard_normal(out[name].shape)
        drawn = base * np.exp(spread * noise) if base else spread * noise
        out[name] = jnp.asarray(drawn.astype(out[name].dtype))
    for name, factor in factors.items():
        out[name] = (out[name] * factor).astype(out[name].dtype)
    return out
```

```python
from contextlib import ExitStack

import numpy as np

import concourse.bass as bass
import concourse.mybir as mybir

F32 = mybir.dt.float32
ALU = mybir.AluOpType
ACT = mybir.ActivationFunctionType
AX_X = mybir.AxisListType.X

P = 128
BATCH, SEQ = 32, 32
HEADS, CH = 16, 8
SEQ_PER_TILE = P // SEQ
TILES = BATCH * SEQ // P
GROUPS = 4
HPG = HEADS // GROUPS
QUAD = 32
EPS = 1e-6
Q_LOW = P // CH
Q_HIGH = SEQ // Q_LOW
VW = CH + 1
FF = (4, 2)
GELU = (ACT.Gelu_apprx_tanh, ACT.Gelu)
SCORE_SCALE = (1.0 / CH, 1.0 / float(np.sqrt(np.float32(CH))))

CHUNKS = 2
CT = TILES // CHUNKS
CW = CT * P
CSEQ = CT * SEQ_PER_TILE
HALF = 2
HALVES = CT // HALF

COND0 = 0
MASK0 = COND0 + BATCH
IDENT0 = MASK0 + HPG
BIAS0 = IDENT0 + P
B_ADA = (BIAS0, BIAS0 + 6)
B_O = (BIAS0 + 12, BIAS0 + 13)
B_FF1 = (BIAS0 + 14, BIAS0 + 18)
B_FF2 = (BIAS0 + 20, BIAS0 + 21)
B_Q, B_K, B_V = BIAS0 + 22, BIAS0 + 23, BIAS0 + 24
VEC_COLS = BIAS0 + 25

W_ADA, W_Q, W_K, W_V = 0, 6 * P, 7 * P, 8 * P
W_O, W_FF1 = 9 * P, 10 * P
W_FF2 = tuple(W_FF1 + f * P for f in FF)
W_COLS = tuple(W_FF2[n] + FF[n] * P for n in range(2))
W_FIRST = 9 * P

SHIFT, SCALE, GATE = 0, 1, 2


def block_steps(layer, chunk):
    def norm(part):
        return [(("stat", layer, chunk, part), 1.0), (("hat", layer, chunk, part), 1.0),
                (("mod", layer, chunk, part), 1.0)]

    steps = norm(0) + [(("kqv", layer, chunk, 0), 2.0)]
    if chunk == 0:
        steps.insert(1, (("ada", layer, chunk, 0), 1.0))
    for g in range(GROUPS):
        steps.append((("scores", layer, chunk, g), 2.0))
        if g:
            steps.append((("turn", layer, chunk, g - 1), 1.0))
    steps.append((("turn", layer, chunk, GROUPS - 1), 1.0))
    steps += [(("pv", layer, chunk, h), 1.0) for h in range(HALVES)]
    steps += [(("fold", layer, chunk, 0), FOLD_GAP[layer]), (("proj", layer, chunk, 0), 1.0), (("gate", layer, chunk, 0), 1.0), (("res", layer, chunk, 0), 1.0)]
    steps += norm(1)
    steps += [(("ff1", layer, chunk, f), 1.0) for f in range(FF[layer])]
    steps += [(("ff2", layer, chunk, 0), 1.0), (("gate", layer, chunk, 1), 1.0), (("res", layer, chunk, 1), 1.0)]
    return steps


FOLD_GAP = (1.0, 4.0)
LAG = 18.0


def schedule():
    keyed = []
    for chunk in range(CHUNKS):
        at = LAG * chunk
        for layer in range(2):
            for step, weight in block_steps(layer, chunk):
                keyed.append((at, chunk, step))
                at += weight
    return [step for _, _, step in sorted(keyed)]


SCHEDULE = schedule()


def nth(step):
    return sum(s[0] == step[0] for s in SCHEDULE[:SCHEDULE.index(step) + 1])


def lin_uses(step):
    return {"kqv": 3, "ff1": 1}.get(step[0], 0)


def vec_uses(step):
    return {"ada": 1, "hat": 1, "pv": 1, "proj": 1, "gate": 1, "ff2": 1}.get(step[0], 0)


def lin_before(step):
    return sum(lin_uses(s) for s in SCHEDULE[:SCHEDULE.index(step)])


def vec_before(step):
    return sum(vec_uses(s) for s in SCHEDULE[:SCHEDULE.index(step)] if s[2] == step[2])


def earlier(kind, layer, chunk, part):
    if part:
        return (kind, layer, chunk, 0)
    return (kind, layer - 1, chunk, 1) if layer else None


LIN_BANKS, SCORE_BANKS = 2, 2
VEC_BANKS = 4 // CHUNKS


def two_blocks(nc, x, vectors, weights0, weights1, scratch, out):
    with ExitStack() as ctx:
        def sb(name, shape):
            return ctx.enter_context(nc.sbuf_tensor(name, shape, F32))

        def bank(name):
            return ctx.enter_context(nc.psum_tensor(name, [P, 512], F32))

        def sem(name):
            return ctx.enter_context(nc.semaphore(name))

        x_tok = sb("x_tok", [P, TILES, P])
        vec = sb("vec", [P, VEC_COLS])
        w = [sb("w0", [P, W_COLS[0]]), sb("w1", [P, W_COLS[1]])]
        e_cond = sb("e_cond", [P, BATCH])
        s_cond = sb("s_cond", [P, BATCH])
        ada = sb("ada", [P, 2, 6, BATCH])
        b_ada1 = sb("b_ada1", [P, 2, 6])
        bk_mask = sb("bk_mask", [P, HPG])
        half_neg = sb("half_neg", [P, CT])
        stats = sb("stats", [P, CHUNKS, CT, 6])
        mean_var = sb("mean_var", [P, CHUNKS, CT, 2])
        var_eps = sb("var_eps", [P, CHUNKS, CT])
        rstd = sb("rstd", [P, CHUNKS, CT])
        x_hat = sb("x_hat", [P, CHUNKS, CT, P])
        x_mod = sb("x_mod", [P, CHUNKS, CW])
        qT = sb("qT", [P, CHUNKS, CW])
        kT_mask = sb("kT_mask", [P, CHUNKS, HPG, CW])
        v_own = sb("v_own", [P, CHUNKS, CT, HEADS, SEQ_PER_TILE, VW])
        row_max = sb("row_max", [P, CHUNKS, GROUPS, CT * HPG])
        probs = sb("probs", [P, CHUNKS, GROUPS, CW])
        probs_T = sb("probs_T", [P, CHUNKS, GROUPS, CW])
        sum_inv = sb("sum_inv", [P, CHUNKS, HALVES, HALF * HEADS])
        att = sb("att", [P, CHUNKS, CW])
        att_T = sb("att_T", [P, CHUNKS, CW])
        att_rows = sb("att_rows", [P, CHUNKS, HEADS, CW // Q_LOW])
        gated = sb("gated", [P, CHUNKS, CW])
        hidden = sb("hidden", [P, CHUNKS, max(FF), CW])

        lin = [bank(f"lin{n}") for n in range(LIN_BANKS)]
        vecb = [bank(f"vecb{n}") for n in range(CHUNKS * VEC_BANKS)]
        scb = [bank(f"scb{n}") for n in range(SCORE_BANKS)]

        x_in = [sem(f"x_in{c}") for c in range(CHUNKS)]
        vec_in = sem("vec_in")
        w_first_in = [sem("w0_first_in"), sem("w1_first_in")]
        w_rest_in = [sem("w0_rest_in"), sem("w1_rest_in")]
        exp_cond = sem("exp_cond")
        cond_step = sem("cond_step")
        cond_ready = sem("cond_ready")
        consts_ready = sem("consts_ready")
        ada_ready = sem("ada_ready")
        exponent_ready = sem("exponent_ready")
        v_zeroed = sem("v_zeroed")
        v_ones = sem("v_ones")
        stats_done = sem("stats_done")
        aggr_done = sem("aggr_done")
        var_ready = sem("var_ready")
        rstd_ready = sem("rstd_ready")
        hat_ready = sem("hat_ready")
        mod_ready = sem("mod_ready")
        lin_ready = sem("lin_ready")
        lin_taken = sem("lin_taken")
        vec_ready = [sem(f"vec_ready{c}") for c in range(CHUNKS)]
        vec_taken = [sem(f"vec_taken{c}") for c in range(CHUNKS)]
        scores_ready = sem("scores_ready")
        scores_taken = sem("scores_taken")
        max_ready = sem("max_ready")
        probs_ready = sem("probs_ready")
        probs_turned = sem("probs_turned")
        inv_ready = sem("inv_ready")
        att_turned = sem("att_turned")
        att_folded = sem("att_folded")
        att_sent = [sem(f"att_sent{c}") for c in range(CHUNKS)]
        att_back = [sem(f"att_back{c}") for c in range(CHUNKS)]
        x_updated = sem("x_updated")
        out_done = sem("out_done")

        ident = vec[:, IDENT0:IDENT0 + P]

        def column(n):
            return vec[:, n:n + 1]

        def lin_bank(use):
            return lin[use % LIN_BANKS]

        def vec_bank(chunk, use):
            return vecb[VEC_BANKS * chunk + use % VEC_BANKS]

        def by_seq(ap):
            return ap.rearrange("p (s k) -> p s k", k=SEQ)

        def ada_of(layer, which, chunk):
            v = ada[:, layer, which, CSEQ * chunk:CSEQ * (chunk + 1)]
            return v.unsqueeze(2).broadcast_to([P, CSEQ, SEQ])

        block = ctx.enter_context(nc.Block())

        @block.sync
        def _(sp):
            sp.dma_start(vec[:], vectors).then_inc(vec_in, 16)
            sp.dma_start(w[0][:, 0:W_FIRST], weights0[:, 0:W_FIRST]).then_inc(w_first_in[0], 16)
            for c in range(CHUNKS):
                sp.dma_start(x_tok[:, CT * c:CT * (c + 1), :],
                             x[:, CW * c:CW * (c + 1)].rearrange("p (t f) -> p t f", f=P)).then_inc(x_in[c], 16)
            sp.dma_start(w[0][:, W_FIRST:], weights0[:, W_FIRST:]).then_inc(w_rest_in[0], 16)
            sp.dma_start(w[1][:, 0:W_FIRST], weights1[:, 0:W_FIRST]).then_inc(w_first_in[1], 16)
            sp.dma_start(w[1][:, W_FIRST:], weights1[:, W_FIRST:]).then_inc(w_rest_in[1], 16)
            for c in range(CHUNKS):
                sp.wait_ge(att_folded, nth(("fold", 1, c, 0)))
                sp.dma_start(scratch[c].rearrange("h c l n -> (h c) (l n)"), att_T[:, c]).then_inc(att_sent[c], 16)
                sp.wait_ge(att_sent[c], 16)
                sp.dma_start(att_rows[:, c], scratch[c].rearrange("h c l n -> (c l) h n")).then_inc(att_back[c], 16)
            for c in range(CHUNKS):
                sp.wait_ge(x_updated, nth(("res", 1, c, 1)))
                sp.dma_start(out[:, CW * c:CW * (c + 1)],
                             x_tok[:, CT * c:CT * (c + 1), :].rearrange("p t f -> p (t f)")).then_inc(out_done, 16)
            sp.wait_ge(out_done, 16 * CHUNKS)

        @block.gpsimd
        def _(pool):
            pool.memset(half_neg[:], -0.5).then_inc(exponent_ready, 1)
            for c in range(CHUNKS):
                pool.memset(v_own[:, c], 0.0).then_inc(v_zeroed, 1)
            pool.wait_ge(v_zeroed, CHUNKS)
            for b in range(SEQ_PER_TILE):
                rows = slice(QUAD * b, QUAD * (b + 1))
                pool.memset(v_own[rows, :, :, :, b, CH:VW], 1.0).then_inc(v_ones, 1)
                pool.wait_ge(v_ones, b + 1)

            def stat(step, layer, c, part):
                pool.wait_ge(var_ready, nth(step))
                pool.wait_ge(exponent_ready, 1)
                if earlier("hat", layer, c, part):
                    pool.wait_ge(hat_ready, nth(earlier("hat", layer, c, part)))
                pool.tensor_tensor(rstd[:, c], var_eps[:, c], half_neg[:], ALU.pow).then_inc(rstd_ready, 1)

            def mod(step, layer, c, part):
                pool.wait_ge(vec_taken[c], vec_before(("hat", layer, c, part)) + 1)
                pool.tensor_tensor(by_seq(x_mod[:, c]), by_seq(x_mod[:, c]), ada_of(layer, 3 * part + SHIFT, c),
                                   ALU.add).then_inc(mod_ready, 1)

            for step in SCHEDULE:
                if step[0] == "stat":
                    stat(step, *step[1:])
                if step[0] == "mod":
                    mod(step, *step[1:])

        @block.scalar
        def _(act):
            act.wait_ge(vec_in, 16)
            act.activation(e_cond[:], vec[:, COND0:COND0 + BATCH], ACT.Exp, scale=-1.0).then_inc(exp_cond, 1)
            act.wait_ge(consts_ready, 2)

            def kqv(step, layer, c, _):
                use = lin_before(step)
                act.wait_ge(lin_ready, use + 1)
                if layer:
                    act.wait_ge(scores_ready, nth(("scores", layer - 1, c, GROUPS - 1)))
                for h in range(HPG):
                    bias = bk_mask[:, h:h + 1] if layer else 0.0
                    last = act.activation(kT_mask[:, c, h], lin_bank(use)[:, 0:CW], ACT.Identity,
                                          scale=column(MASK0 + h), bias=bias)
                last.then_inc(lin_taken, 1)
                act.wait_ge(lin_ready, use + 2)
                act.activation(qT[:, c], lin_bank(use + 1)[:, 0:CW], ACT.Identity,
                               bias=column(B_Q) if layer else 0.0).then_inc(lin_taken, 1)
                act.wait_ge(lin_ready, use + 3)
                if layer:
                    act.wait_ge(vec_ready[c], vec_before(("pv", layer - 1, c, HALVES - 1)) + 1)
                else:
                    act.wait_ge(v_ones, SEQ_PER_TILE)
                for b in range(SEQ_PER_TILE):
                    rows = slice(QUAD * b, QUAD * (b + 1))
                    last = act.activation(v_own[rows, c, :, :, b, 0:CH].rearrange("p t h c -> p (t h) c"),
                                          lin_bank(use + 2)[rows, 0:CW].rearrange("p (n c) -> p n c", c=CH),
                                          ACT.Identity)
                last.then_inc(lin_taken, 1)

            def scores(step, layer, c, g):
                act.wait_ge(scores_taken, nth(step))
                act.activation(probs[:, c, g], probs[:, c, g], ACT.Exp,
                               scale=SCORE_SCALE[layer]).then_inc(probs_ready, 1)

            def ff1(step, layer, c, f):
                use = lin_before(step)
                act.wait_ge(lin_ready, use + 1)
                if layer:
                    act.wait_ge(vec_ready[c], vec_before(("ff2", layer - 1, c, 0)) + 1)
                act.activation(hidden[:, c, f], lin_bank(use)[:, 0:CW], GELU[layer],
                               bias=column(B_FF1[layer] + f)).then_inc(lin_taken, 1)

            for step in SCHEDULE:
                if step[0] == "kqv":
                    kqv(step, *step[1:])
                if step[0] == "scores":
                    scores(step, *step[1:])
                if step[0] == "ff1":
                    ff1(step, *step[1:])

        @block.vector
        def _(dve):
            dve.wait_ge(vec_in, 16)
            dve.tensor_scalar(bk_mask[:], vec[:, MASK0:MASK0 + HPG], column(B_K), None, ALU.mult).then_inc(consts_ready, 1)
            dve.tensor_copy(b_ada1[:].rearrange("p l n -> p (l n)"), vec[:, BIAS0:BIAS0 + 12]).then_inc(consts_ready, 1)
            dve.wait_ge(consts_ready, 2)
            dve.tensor_scalar(b_ada1[:, :, SCALE::3], b_ada1[:, :, SCALE::3], 1.0, None, ALU.add).then_inc(consts_ready, 1)
            dve.wait_ge(exp_cond, 1)
            dve.tensor_scalar(e_cond[:], e_cond[:], 1.0, None, ALU.add).then_inc(cond_step, 1)
            dve.wait_ge(cond_step, 1)
            dve.reciprocal(e_cond[:], e_cond[:]).then_inc(cond_step, 1)
            dve.wait_ge(cond_step, 2)
            dve.tensor_tensor(s_cond[:], e_cond[:], vec[:, COND0:COND0 + BATCH], ALU.mult).then_inc(cond_ready, 1)
            dve.wait_ge(consts_ready, 3)

            def ada_vectors(step, layer, c, _):
                use = vec_before(step)
                src = vec_bank(c, use)
                dve.wait_ge(vec_ready[c], use + 1)
                dve.tensor_tensor(ada[:, layer], src[:, 0:6 * BATCH].rearrange("p (n b) -> p n b", b=BATCH),
                                  b_ada1[:, layer].unsqueeze(2).broadcast_to([P, 6, BATCH]),
                                  ALU.add).then_inc(ada_ready, 1)
                dve.wait_ge(ada_ready, layer + 1)
                dve.sem_inc(vec_taken[c], 1)

            def stat(step, layer, c, part):
                if earlier("res", layer, c, part):
                    dve.wait_ge(x_updated, nth(earlier("res", layer, c, part)))
                else:
                    dve.wait_ge(x_in[c], 16)
                for t in range(CT):
                    dve.bn_stats(stats[:, c, t], x_tok[:, CT * c + t]).then_inc(stats_done, 1)
                dve.wait_ge(stats_done, CT * nth(step))
                for t in range(CT):
                    dve.bn_aggr(mean_var[:, c, t], stats[:, c, t]).then_inc(aggr_done, 1)
                dve.wait_ge(aggr_done, CT * nth(step))
                dve.tensor_scalar(var_eps[:, c], mean_var[:, c, :, 1], EPS, None, ALU.add).then_inc(var_ready, 1)

            def hat(step, layer, c, part):
                dve.wait_ge(rstd_ready, nth(("stat", layer, c, part)))
                if earlier("hat", layer, c, part):
                    dve.wait_ge(vec_ready[c], vec_before(earlier("hat", layer, c, part)) + 1)
                for t in range(CT):
                    last = dve.tensor_scalar(x_hat[:, c, t], x_tok[:, CT * c + t], mean_var[:, c, t, 0:1],
                                             rstd[:, c, t:t + 1], ALU.subtract, ALU.mult)
                last.then_inc(hat_ready, 1)

            def mod(step, layer, c, part):
                use = vec_before(("hat", layer, c, part))
                dve.wait_ge(vec_ready[c], use + 1)
                dve.wait_ge(ada_ready, layer + 1)
                if part:
                    dve.wait_ge(lin_ready, lin_before(("kqv", layer, c, 0)) + 3)
                elif layer:
                    dve.wait_ge(lin_ready, lin_before(("ff1", layer - 1, c, FF[layer - 1] - 1)) + 1)
                dve.tensor_tensor(by_seq(x_mod[:, c]), by_seq(vec_bank(c, use)[:, 0:CW]),
                                  ada_of(layer, 3 * part + SCALE, c), ALU.mult).then_inc(vec_taken[c], 1)

            def scores(step, layer, c, g):
                n = nth(step)
                src = scb[(n - 1) % SCORE_BANKS][:, 0:CW].rearrange("p (n k) -> p n k", k=SEQ)
                dve.wait_ge(scores_ready, n)
                dve.tensor_reduce(row_max[:, c, g], src, AX_X, ALU.max).then_inc(max_ready, 1)
                dve.wait_ge(max_ready, n)
                dve.tensor_tensor(probs[:, c, g].rearrange("p (n k) -> p n k", k=SEQ), src,
                                  row_max[:, c, g].unsqueeze(2).broadcast_to([P, CT * HPG, SEQ]),
                                  ALU.subtract).then_inc(scores_taken, 1)

            def turn(step, layer, c, g):
                dve.wait_ge(probs_ready, nth(("scores", layer, c, g)))
                if layer:
                    dve.wait_ge(vec_ready[c], vec_before(("pv", layer - 1, c, HALVES - 1)) + 1)
                dve.transpose(probs_T[:, c, g], probs[:, c, g]).then_inc(probs_turned, 1)

            def pv(step, layer, c, half):
                use = vec_before(step)
                src = vec_bank(c, use)[:, 0:HALF * HEADS * VW].rearrange("p (n w) -> p n w", w=VW)
                dve.wait_ge(vec_ready[c], use + 1)
                dve.reciprocal(sum_inv[:, c, half], src[:, :, CH]).then_inc(inv_ready, 1)
                dve.wait_ge(inv_ready, nth(step))
                dst = att[:, c, HALF * P * half:HALF * P * (half + 1)].rearrange("p (n w) -> p n w", w=CH)
                dve.tensor_tensor(dst, src[:, :, 0:CH],
                                  sum_inv[:, c, half].unsqueeze(2).broadcast_to([P, HALF * HEADS, CH]),
                                  ALU.mult).then_inc(vec_taken[c], 1)

            def fold(step, layer, c, _):
                dve.wait_ge(vec_taken[c], vec_before(step))
                if layer:
                    dve.wait_ge(vec_ready[c], vec_before(("proj", layer - 1, c, 0)) + 1)
                    src = att_T[:, c].rearrange("p (l s e) -> p s e l", l=Q_LOW, e=Q_HIGH)
                    dve.transpose(src, att[:, c]).then_inc(att_turned, 1)
                    dve.wait_ge(att_turned, nth(step))
                    dve.tensor_scalar(att_T[:, c], att_T[:, c], column(B_V), None, ALU.add).then_inc(att_folded, 1)
                else:
                    dve.transpose(att_T[:, c], att[:, c]).then_inc(att_turned, 1)
                    dve.wait_ge(att_turned, nth(step))
                    dve.sem_inc(att_folded, 1)

            def gate(step, layer, c, part):
                use = vec_before(("ff2" if part else "proj", layer, c, 0))
                dve.wait_ge(vec_ready[c], use + 1)
                bias = column(B_FF2[layer] if part else B_O[layer])
                if earlier("gate", layer, c, part):
                    dve.wait_ge(vec_ready[c], vec_before(earlier("gate", layer, c, part)) + 1)
                dve.scalar_tensor_tensor(by_seq(gated[:, c]), by_seq(vec_bank(c, use)[:, 0:CW]), bias,
                                         ada_of(layer, 3 * part + GATE, c), ALU.add,
                                         ALU.mult).then_inc(vec_taken[c], 1)

            def res(step, layer, c, part):
                use = vec_before(("gate", layer, c, part))
                dve.wait_ge(vec_ready[c], use + 1)
                tokens = x_tok[:, CT * c:CT * (c + 1)].rearrange("p t f -> p (t f)")
                dve.tensor_tensor(tokens, tokens, vec_bank(c, use)[:, 0:CW], ALU.add).then_inc(x_updated, 1)
                dve.wait_ge(x_updated, nth(step))
                dve.sem_inc(vec_taken[c], 1)

            parts = {"ada": ada_vectors, "stat": stat, "hat": hat, "mod": mod, "scores": scores, "turn": turn,
                     "pv": pv, "fold": fold, "gate": gate, "res": res}
            for step in SCHEDULE:
                if step[0] in parts:
                    parts[step[0]](step, *step[1:])

        @block.tensor
        def _(pe):
            def free_bank(c, use):
                if use >= VEC_BANKS:
                    pe.wait_ge(vec_taken[c], use - VEC_BANKS + 1)
                return vec_bank(c, use)

            def free_lin(use):
                if use >= LIN_BANKS:
                    pe.wait_ge(lin_taken, use - LIN_BANKS + 1)
                return lin_bank(use)

            def ada_vectors(step, layer, c, _):
                dst = free_bank(c, vec_before(step))
                pe.wait_ge(cond_ready, 1)
                pe.wait_ge(w_first_in[layer], 16)
                for n in range(6):
                    last = pe.matmul(dst[:, BATCH * n:BATCH * (n + 1)], w[layer][:, W_ADA + P * n:W_ADA + P * (n + 1)],
                                     s_cond[:], start=True, stop=True)
                last.then_inc(vec_ready[c], 1)

            def turn_tiles(dst, src, done):
                for t in range(CT):
                    last = pe.transpose(dst[:, P * t:P * (t + 1)], src(t), ident)
                last.then_inc(done, 1)

            def hat(step, layer, c, part):
                pe.wait_ge(vec_in, 16)
                pe.wait_ge(hat_ready, nth(step))
                turn_tiles(free_bank(c, vec_before(step)), lambda t: x_hat[:, c, t], vec_ready[c])

            def kqv(step, layer, c, _):
                use = lin_before(step)
                pe.wait_ge(mod_ready, nth(("mod", layer, c, 0)))
                pe.wait_ge(w_first_in[layer], 16)
                for n, at in ((0, W_K), (1, W_Q)):
                    pe.matmul(free_lin(use + n)[:, 0:CW], w[layer][:, at:at + P], x_mod[:, c],
                              start=True, stop=True).then_inc(lin_ready, 1)
                dst = free_lin(use + 2)
                for t in range(CT):
                    last = pe.matmul(dst[:, P * t:P * (t + 1)], x_mod[:, c, P * t:P * (t + 1)],
                                     w[layer][:, W_V:W_V + P], start=True, stop=True)
                last.then_inc(lin_ready, 1)

            def scores(step, layer, c, g):
                n = nth(step)
                pe.wait_ge(lin_taken, lin_before(("kqv", layer, c, 0)) + 2)
                if n > SCORE_BANKS:
                    pe.wait_ge(scores_taken, n - SCORE_BANKS)
                rows = slice(QUAD * g, QUAD * (g + 1))
                for t in range(CT):
                    for b in range(SEQ_PER_TILE):
                        seq = slice(P * t + SEQ * b, P * t + SEQ * (b + 1))
                        last = pe.matmul(scb[(n - 1) % SCORE_BANKS][QUAD * b:QUAD * (b + 1), P * t:P * (t + 1)],
                                         qT[rows, c, seq], kT_mask[rows, c, :, seq], start=True, stop=True)
                last.then_inc(scores_ready, 1)

            def pv(step, layer, c, half):
                pe.wait_ge(probs_turned, nth(("turn", layer, c, GROUPS - 1)))
                pe.wait_ge(lin_taken, lin_before(("kqv", layer, c, 0)) + 3)
                dst = free_bank(c, vec_before(step))[:, 0:HALF * HEADS * VW].rearrange(
                    "p (t b h w) -> p t b h w", t=HALF, b=SEQ_PER_TILE, w=VW)
                for t in range(HALF):
                    for h in range(HPG):
                        for g in range(GROUPS):
                            tile = HALF * half + t
                            q = slice(P * tile + SEQ * h, P * tile + SEQ * (h + 1))
                            last = pe.matmul(dst[QUAD * g:QUAD * (g + 1), t, :, h, :], probs_T[:, c, g, q],
                                             v_own[:, c, tile, HPG * g + h], start=True, stop=True)
                last.then_inc(vec_ready[c], 1)

            def proj(step, layer, c, _):
                pe.wait_ge(w_rest_in[layer], 16)
                if layer:
                    pe.wait_ge(att_back[c], 16)
                    src = att_rows[:, c].rearrange("p h (s e) -> p s h e", e=Q_HIGH)
                else:
                    pe.wait_ge(att_folded, nth(("fold", layer, c, 0)))
                    src = att_T[:, c]
                pe.matmul(free_bank(c, vec_before(step))[:, 0:CW], w[layer][:, W_O:W_O + P], src,
                          start=True, stop=True).then_inc(vec_ready[c], 1)

            def gate(step, layer, c, part):
                source = ("ff2" if part else "proj", layer, c, 0)
                pe.wait_ge(vec_taken[c], vec_before(source) + 1)
                turn_tiles(free_bank(c, vec_before(step)), lambda t: gated[:, c, P * t:P * (t + 1)], vec_ready[c])

            def ff1(step, layer, c, f):
                pe.wait_ge(mod_ready, nth(("mod", layer, c, 1)))
                at = W_FF1 + P * f
                pe.matmul(free_lin(lin_before(step))[:, 0:CW], w[layer][:, at:at + P], x_mod[:, c],
                          start=True, stop=True).then_inc(lin_ready, 1)

            def ff2(step, layer, c, _):
                dst = free_bank(c, vec_before(step))
                for f in range(FF[layer]):
                    pe.wait_ge(lin_taken, lin_before(("ff1", layer, c, f)) + 1)
                    at = W_FF2[layer] + P * f
                    last = pe.matmul(dst[:, 0:CW], w[layer][:, at:at + P], hidden[:, c, f],
                                     start=f == 0, stop=f == FF[layer] - 1)
                last.then_inc(vec_ready[c], 1)

            parts = {"ada": ada_vectors, "hat": hat, "kqv": kqv, "scores": scores, "pv": pv, "proj": proj,
                     "gate": gate, "ff1": ff1, "ff2": ff2}
            for step in SCHEDULE:
                if step[0] in parts:
                    parts[step[0]](step, *step[1:])


def kernel(**inputs):
    import concourse.bacc as bacc
    from concourse.bass_utils import run_bass_kernel_spmd

    a = {name: np.asarray(value) for name, value in inputs.items()}
    l0 = {k[8:]: v for k, v in a.items() if k.startswith("L0_cond_")}
    l1 = {k[8:]: v for k, v in a.items() if k.startswith("L1_cond_")}
    f32 = np.float32

    def columns(v):
        return v.reshape(-1, P).T

    def down(v):
        return v.reshape(-1, P, P).transpose(1, 0, 2).reshape(P, -1)

    masks = (np.arange(P)[:, None] // CH % HPG == np.arange(HPG)[None, :]).astype(f32)
    vectors = np.concatenate(
        [a["cond_1024"].T, masks, np.eye(P, dtype=f32), columns(l0["b_ada"]), columns(l1["bada"]),
         columns(l0["b_proj"]), columns(l1["bo"]), columns(l0["b_mlp1"]), columns(l1["b1"]),
         columns(l0["b_mlp2"]), columns(l1["b2"]), columns(l1["bq"]), columns(l1["bk"]), columns(l1["bv"])], axis=1)
    w_k, w_q, w_v = np.split(l0["w_qkv"], 3, axis=1)
    weights0 = np.concatenate([l0["w_ada"], w_q, w_k, w_v, l0["w_proj"], l0["w_mlp1"], down(l0["w_mlp2"])], axis=1)
    w_o1 = l1["Wo"].reshape(P // CH, CH, P).transpose(1, 0, 2).reshape(P, P)
    weights1 = np.concatenate([l1["Wada"], l1["Wq"], l1["Wk"], l1["Wv"], w_o1, l1["W1"], down(l1["W2"])], axis=1)
    arrays = {
        "x": np.ascontiguousarray(a["x"].reshape(TILES, P, P).transpose(1, 0, 2).reshape(P, -1)),
        "vectors": np.ascontiguousarray(vectors),
        "weights0": np.ascontiguousarray(weights0),
        "weights1": np.ascontiguousarray(weights1),
    }
    nc = bacc.Bacc("TRN2", target_bir_lowering=False, num_devices=1)
    args = [nc.dram_tensor(f"{name}_dram", v.shape, F32, kind="ExternalInput").ap() for name, v in arrays.items()]
    out = nc.dram_tensor("out_dram", (P, TILES * P), F32, kind="ExternalOutput").ap()
    scratch = nc.dram_tensor("scratch_dram", (CHUNKS, HEADS, CH, Q_LOW, CW // Q_LOW), F32, kind="Internal").ap()
    two_blocks(nc, *args, scratch, out)
    r = run_bass_kernel_spmd(nc, [{f"{name}_dram": v for name, v in arrays.items()}], core_ids=[0])
    y = r.results[0]["out_dram"]
    return np.asarray(y).reshape(P, TILES, P).transpose(1, 0, 2).reshape(BATCH, SEQ, P)
```

```python
from contextlib import ExitStack

import numpy as np

import concourse.bass as bass
import concourse.mybir as mybir

F32 = mybir.dt.float32
ALU = mybir.AluOpType
ACT = mybir.ActivationFunctionType
AX_X = mybir.AxisListType.X

P = 128
BATCH, SEQ = 32, 32
HEADS, CH = 16, 8
SEQ_PER_TILE = P // SEQ
TILES = BATCH * SEQ // P
GROUPS = 4
HPG = HEADS // GROUPS
QUAD = 32
EPS = 1e-6
Q_LOW = P // CH
Q_HIGH = SEQ // Q_LOW
VW = CH + 1
FF = (4, 2)
GELU = (ACT.Gelu_apprx_tanh, ACT.Gelu)
SCORE_SCALE = (1.0 / CH, 1.0 / float(np.sqrt(np.float32(CH))))

CHUNKS = 4
CT = TILES // CHUNKS
CW = CT * P
CSEQ = CT * SEQ_PER_TILE
HALF = 2
HALVES = CT // HALF

COND0 = 0
MASK0 = COND0 + BATCH
IDENT0 = MASK0 + HPG
BIAS0 = IDENT0 + P
B_ADA = (BIAS0, BIAS0 + 6)
B_O = (BIAS0 + 12, BIAS0 + 13)
B_FF1 = (BIAS0 + 14, BIAS0 + 18)
B_FF2 = (BIAS0 + 20, BIAS0 + 21)
B_Q, B_K, B_V = BIAS0 + 22, BIAS0 + 23, BIAS0 + 24
VEC_COLS = BIAS0 + 25

W_ADA, W_Q, W_K, W_V = 0, 6 * P, 7 * P, 8 * P
W_O, W_FF1 = 9 * P, 10 * P
W_FF2 = tuple(W_FF1 + f * P for f in FF)
W_COLS = tuple(W_FF2[n] + FF[n] * P for n in range(2))
W_FIRST = 9 * P

SHIFT, SCALE, GATE = 0, 1, 2


DUE = (
    {
        "cond": [2.1],
        "ada": [3.38],
        "stat": [-0.13, 32.21],
        "rstd": [4.71, 32.54],
        "hat": [3.14, 35.37],
        "turn_hat": [2.95, 36.72],
        "mod": [5.65, 37.37],
        "shift": [4.89, 35.19],
        "k": [6.44],
        "q": [7.46],
        "v": [8.94],
        "mask_k": [9.5],
        "copy_q": [8.37],
        "copy_v": [11.65],
        "scores": [12.0, 13.5, 15.05, 16.46],
        "max": [12.9, 15.05, 15.54, 17.9],
        "sub": [13.9, 15.53, 16.95, 18.76],
        "exp": [14.62, 15.11, 17.25, 18.45],
        "turn": [15.28, 17.87, 18.66, 20.05],
        "pv": [21.08],
        "norm": [24.56],
        "fold": [27.51],
        "proj": [28.25],
        "gate": [29.2, 46.62],
        "turn_gate": [30.21, 47.79],
        "res": [31.02, 46.86],
        "ff1": [39.3, 40.3, 41.99, 42.3],
        "gelu": [36.38, 39.89, 42.41, 43.18],
        "ff2": [44.71],
    },
    {
        "cond": [0.99],
        "ada": [1.32],
        "stat": [-2.46, 37.53],
        "rstd": [2.08, 40.73],
        "hat": [3.4, 37.53],
        "turn_hat": [4.0, 39.26],
        "mod": [5.11, 40.09],
        "shift": [9.03, 42.42],
        "k": [7.24],
        "q": [8.56],
        "v": [11.44],
        "mask_k": [7.43],
        "copy_q": [11.15],
        "copy_v": [14.26],
        "scores": [12.25, 14.44, 15.12, 17.43],
        "max": [13.47, 14.97, 16.47, 18.14],
        "sub": [13.84, 15.69, 17.19, 18.95],
        "exp": [15.09, 15.98, 18.09, 19.11],
        "turn": [15.79, 17.59, 18.81, 19.97],
        "pv": [22.37],
        "norm": [23.86],
        "fold": [27.94],
        "proj": [34.44],
        "gate": [35.04, 48.71],
        "turn_gate": [35.96, 49.39],
        "res": [37.51, 49.82],
        "ff1": [41.99, 43.85],
        "gelu": [38.02, 43.89],
        "ff2": [45.25],
    },
)
BLOCK = 50.14
LAG = 4.62
ONCE = ("cond", "ada")


def schedule():
    due = []
    for chunk in range(CHUNKS):
        for layer in range(2):
            for kind, times in DUE[layer].items():
                if kind not in ONCE or chunk == 0:
                    due += [(at + BLOCK * layer + LAG * chunk, chunk, (kind, layer, chunk, part))
                            for part, at in enumerate(times)]
    steps = [step for _, _, step in sorted(due, key=lambda d: d[:2])]
    in_written_order(steps, LIN_READER)
    in_written_order(steps, {"scores": "max"})
    in_written_order(steps, {"scores": "sub"})
    return steps


def in_written_order(steps, reader):
    wanted = [(reader[s[0]],) + s[1:] for s in steps if s[0] in reader]
    places = [i for i, s in enumerate(steps) if s[0] in reader.values()]
    for place, step in zip(places, wanted):
        steps[place] = step


LIN_READER = {"k": "mask_k", "q": "copy_q", "v": "copy_v", "ff1": "gelu"}
SCHEDULE = schedule()


def nth(kind, layer, chunk, part=0):
    at = SCHEDULE.index((kind, layer, chunk, part))
    return sum(s[0] == kind for s in SCHEDULE[:at + 1])


VEC_WRITERS = ("cond", "turn_hat", "pv", "proj", "turn_gate", "ff2")

def lin_use(*writer):
    return sum(s[0] in LIN_READER for s in SCHEDULE[:SCHEDULE.index(writer)])


def vec_use(*writer):
    return sum(s[0] in VEC_WRITERS and s[2] == writer[2] for s in SCHEDULE[:SCHEDULE.index(writer)])


def taken(*writer):
    return sum(s[0] in VEC_WRITERS and s[0] != "turn_gate" and s[2] == writer[2]
               for s in SCHEDULE[:SCHEDULE.index(writer) + 1])


def before(layer, part):
    if part:
        return layer, 0
    return (layer - 1, 1) if layer else None


LIN_BANKS, SCORE_BANKS = 2, 2
VEC_BANKS = 4 // CHUNKS


def two_blocks(nc, x, vectors, weights0, weights1, scratch, out):
    with ExitStack() as ctx:
        def sb(name, shape):
            return ctx.enter_context(nc.sbuf_tensor(name, shape, F32))

        def bank(name):
            return ctx.enter_context(nc.psum_tensor(name, [P, 512], F32))

        def sem(name):
            return ctx.enter_context(nc.semaphore(name))

        x_tok = sb("x_tok", [P, TILES, P])
        vec = sb("vec", [P, VEC_COLS])
        w = [sb("w0", [P, W_COLS[0]]), sb("w1", [P, W_COLS[1]])]
        e_cond = sb("e_cond", [P, BATCH])
        s_cond = sb("s_cond", [P, BATCH])
        ada = sb("ada", [P, 2, 6, BATCH])
        b_ada1 = sb("b_ada1", [P, 2, 6])
        bk_mask = sb("bk_mask", [P, HPG])
        half_neg = sb("half_neg", [P, CT])
        stats = sb("stats", [P, CHUNKS, CT, 6])
        mean_var = sb("mean_var", [P, CHUNKS, CT, 2])
        var_eps = sb("var_eps", [P, CHUNKS, CT])
        rstd = sb("rstd", [P, CHUNKS, CT])
        x_hat = sb("x_hat", [P, CHUNKS, CT, P])
        x_mod = sb("x_mod", [P, CHUNKS, CW])
        qT = sb("qT", [P, CHUNKS, CW])
        kT_mask = sb("kT_mask", [P, CHUNKS, HPG, CW])
        v_own = sb("v_own", [P, CHUNKS, CT, HEADS, SEQ_PER_TILE, VW])
        row_max = sb("row_max", [P, CHUNKS, GROUPS, CT * HPG])
        probs = sb("probs", [P, CHUNKS, GROUPS, CW])
        probs_T = sb("probs_T", [P, CHUNKS, GROUPS, CW])
        sum_inv = sb("sum_inv", [P, CHUNKS, HALVES, HALF * HEADS])
        att = sb("att", [P, CHUNKS, CW])
        att_T = sb("att_T", [P, CHUNKS, CW])
        att_rows = sb("att_rows", [P, CHUNKS, HEADS, CW // Q_LOW])
        gated = sb("gated", [P, CHUNKS, CW])
        hidden = sb("hidden", [P, CHUNKS, max(FF), CW])

        lin = [bank(f"lin{n}") for n in range(LIN_BANKS)]
        vecb = [bank(f"vecb{n}") for n in range(CHUNKS * VEC_BANKS)]
        scb = [bank(f"scb{n}") for n in range(SCORE_BANKS)]

        x_in = [sem(f"x_in{c}") for c in range(CHUNKS)]
        vec_in = sem("vec_in")
        w_first_in = [sem("w0_first_in"), sem("w1_first_in")]
        w_rest_in = [sem("w0_rest_in"), sem("w1_rest_in")]
        exp_cond = sem("exp_cond")
        cond_step = sem("cond_step")
        cond_ready = sem("cond_ready")
        consts_ready = sem("consts_ready")
        exponent_ready = sem("exponent_ready")
        v_zeroed = sem("v_zeroed")
        v_ones = sem("v_ones")
        stats_done = sem("stats_done")
        aggr_done = sem("aggr_done")
        var_ready = sem("var_ready")
        rstd_ready = sem("rstd_ready")
        hat_ready = sem("hat_ready")
        mod_ready = sem("mod_ready")
        lin_ready = sem("lin_ready")
        lin_taken = sem("lin_taken")
        vec_ready = [sem(f"vec_ready{c}") for c in range(CHUNKS)]
        vec_taken = [sem(f"vec_taken{c}") for c in range(CHUNKS)]
        scores_ready = sem("scores_ready")
        scores_taken = sem("scores_taken")
        max_ready = sem("max_ready")
        probs_ready = sem("probs_ready")
        probs_turned = sem("probs_turned")
        inv_ready = sem("inv_ready")
        att_turned = sem("att_turned")
        att_biased = sem("att_biased")
        att_sent = [sem(f"att_sent{c}") for c in range(CHUNKS)]
        att_back = [sem(f"att_back{c}") for c in range(CHUNKS)]
        x_updated = sem("x_updated")
        out_done = sem("out_done")

        ident = vec[:, IDENT0:IDENT0 + P]

        def column(n):
            return vec[:, n:n + 1]

        def lin_bank(use):
            return lin[use % LIN_BANKS]

        def vec_bank(chunk, use):
            return vecb[VEC_BANKS * chunk + use % VEC_BANKS]

        def by_seq(ap):
            return ap.rearrange("p (s k) -> p s k", k=SEQ)

        def ada_of(layer, which, chunk):
            v = ada[:, layer, which, CSEQ * chunk:CSEQ * (chunk + 1)]
            return v.unsqueeze(2).broadcast_to([P, CSEQ, SEQ])

        def run(parts):
            for kind, layer, chunk, part in SCHEDULE:
                if kind in parts:
                    parts[kind](layer, chunk, part)

        block = ctx.enter_context(nc.Block())

        @block.sync
        def _(sp):
            sp.dma_start(vec[:], vectors).then_inc(vec_in, 16)
            sp.dma_start(w[0][:, 0:W_FIRST], weights0[:, 0:W_FIRST]).then_inc(w_first_in[0], 16)
            for c in range(CHUNKS):
                sp.dma_start(x_tok[:, CT * c:CT * (c + 1), :],
                             x[:, CW * c:CW * (c + 1)].rearrange("p (t f) -> p t f", f=P)).then_inc(x_in[c], 16)
            sp.dma_start(w[0][:, W_FIRST:], weights0[:, W_FIRST:]).then_inc(w_rest_in[0], 16)
            sp.dma_start(w[1][:, 0:W_FIRST], weights1[:, 0:W_FIRST]).then_inc(w_first_in[1], 16)
            sp.dma_start(w[1][:, W_FIRST:], weights1[:, W_FIRST:]).then_inc(w_rest_in[1], 16)
            for c in range(CHUNKS):
                sp.wait_ge(att_biased, sum(s[0] == "fold" and s[1] == 1 for s in SCHEDULE[:SCHEDULE.index(("fold", 1, c, 0)) + 1]))
                sp.dma_start(scratch[c].rearrange("h c l n -> (h c) (l n)"), att_T[:, c]).then_inc(att_sent[c], 16)
                sp.wait_ge(att_sent[c], 16)
                sp.dma_start(att_rows[:, c], scratch[c].rearrange("h c l n -> (c l) h n")).then_inc(att_back[c], 16)
            for c in range(CHUNKS):
                sp.wait_ge(x_updated, nth("res", 1, c, 1))
                sp.dma_start(out[:, CW * c:CW * (c + 1)],
                             x_tok[:, CT * c:CT * (c + 1), :].rearrange("p t f -> p (t f)")).then_inc(out_done, 16)
            sp.wait_ge(out_done, 16 * CHUNKS)

        @block.gpsimd
        def _(pool):
            pool.memset(half_neg[:], -0.5).then_inc(exponent_ready, 1)
            for c in range(CHUNKS):
                pool.memset(v_own[:, c], 0.0).then_inc(v_zeroed, 1)
            pool.wait_ge(v_zeroed, CHUNKS)
            for b in range(SEQ_PER_TILE):
                rows = slice(QUAD * b, QUAD * (b + 1))
                pool.memset(v_own[rows, :, :, :, b, CH:VW], 1.0).then_inc(v_ones, 1)
                pool.wait_ge(v_ones, b + 1)

            def rstd_power(layer, c, part):
                pool.wait_ge(var_ready, nth("stat", layer, c, part))
                pool.wait_ge(exponent_ready, 1)
                if before(layer, part):
                    lb, pb = before(layer, part)
                    pool.wait_ge(hat_ready, nth("hat", lb, c, pb))
                pool.tensor_tensor(rstd[:, c], var_eps[:, c], half_neg[:], ALU.pow).then_inc(rstd_ready, 1)

            def shift(layer, c, part):
                pool.wait_ge(vec_taken[c], taken("turn_hat", layer, c, part))
                pool.tensor_tensor(by_seq(x_mod[:, c]), by_seq(x_mod[:, c]), ada_of(layer, 3 * part + SHIFT, c),
                                   ALU.add).then_inc(mod_ready, 1)

            run({"rstd": rstd_power, "shift": shift})

        @block.scalar
        def _(act):
            act.wait_ge(vec_in, 16)
            act.activation(e_cond[:], vec[:, COND0:COND0 + BATCH], ACT.Exp, scale=-1.0).then_inc(exp_cond, 1)
            act.wait_ge(consts_ready, 2)

            def mask_k(layer, c, _):
                use = lin_use("k", layer, c, 0)
                act.wait_ge(lin_ready, use + 1)
                if layer:
                    act.wait_ge(scores_ready, nth("scores", layer - 1, c, GROUPS - 1))
                for h in range(HPG):
                    last = act.activation(kT_mask[:, c, h], lin_bank(use)[:, 0:CW], ACT.Identity,
                                          scale=column(MASK0 + h), bias=bk_mask[:, h:h + 1] if layer else 0.0)
                last.then_inc(lin_taken, 1)

            def copy_q(layer, c, _):
                use = lin_use("q", layer, c, 0)
                act.wait_ge(lin_ready, use + 1)
                if layer:
                    act.wait_ge(scores_ready, nth("scores", layer - 1, c, GROUPS - 1))
                act.activation(qT[:, c], lin_bank(use)[:, 0:CW], ACT.Identity,
                               bias=column(B_Q) if layer else 0.0).then_inc(lin_taken, 1)

            def copy_v(layer, c, _):
                use = lin_use("v", layer, c, 0)
                act.wait_ge(lin_ready, use + 1)
                if layer:
                    act.wait_ge(vec_ready[c], vec_use("pv", layer - 1, c, HALVES - 1) + 1)
                else:
                    act.wait_ge(v_ones, SEQ_PER_TILE)
                for b in range(SEQ_PER_TILE):
                    rows = slice(QUAD * b, QUAD * (b + 1))
                    last = act.activation(v_own[rows, c, :, :, b, 0:CH].rearrange("p t h c -> p (t h) c"),
                                          lin_bank(use)[rows, 0:CW].rearrange("p (n c) -> p n c", c=CH),
                                          ACT.Identity)
                last.then_inc(lin_taken, 1)

            def exp(layer, c, g):
                act.wait_ge(scores_taken, nth("sub", layer, c, g))
                act.activation(probs[:, c, g], probs[:, c, g], ACT.Exp,
                               scale=SCORE_SCALE[layer]).then_inc(probs_ready, 1)

            def gelu(layer, c, f):
                use = lin_use("ff1", layer, c, f)
                act.wait_ge(lin_ready, use + 1)
                if layer:
                    act.wait_ge(vec_ready[c], vec_use("ff2", layer - 1, c, 0) + 1)
                act.activation(hidden[:, c, f], lin_bank(use)[:, 0:CW], GELU[layer],
                               bias=column(B_FF1[layer] + f)).then_inc(lin_taken, 1)

            run({"mask_k": mask_k, "copy_q": copy_q, "copy_v": copy_v, "exp": exp, "gelu": gelu})

        @block.vector
        def _(dve):
            dve.wait_ge(vec_in, 16)
            dve.tensor_scalar(bk_mask[:], vec[:, MASK0:MASK0 + HPG], column(B_K), None, ALU.mult).then_inc(consts_ready, 1)
            dve.tensor_copy(b_ada1[:].rearrange("p l n -> p (l n)"), vec[:, BIAS0:BIAS0 + 12]).then_inc(consts_ready, 1)
            dve.wait_ge(consts_ready, 2)
            dve.tensor_scalar(b_ada1[:, :, SCALE::3], b_ada1[:, :, SCALE::3], 1.0, None, ALU.add).then_inc(consts_ready, 1)
            dve.wait_ge(exp_cond, 1)
            dve.tensor_scalar(e_cond[:], e_cond[:], 1.0, None, ALU.add).then_inc(cond_step, 1)
            dve.wait_ge(cond_step, 1)
            dve.reciprocal(e_cond[:], e_cond[:]).then_inc(cond_step, 1)
            dve.wait_ge(cond_step, 2)
            dve.tensor_tensor(s_cond[:], e_cond[:], vec[:, COND0:COND0 + BATCH], ALU.mult).then_inc(cond_ready, 1)
            dve.wait_ge(consts_ready, 3)

            def ada_vectors(layer, c, _):
                use = vec_use("cond", layer, c, 0)
                dve.wait_ge(vec_ready[c], use + 1)
                dve.tensor_tensor(ada[:, layer], vec_bank(c, use)[:, 0:6 * BATCH].rearrange("p (n b) -> p n b", b=BATCH),
                                  b_ada1[:, layer].unsqueeze(2).broadcast_to([P, 6, BATCH]),
                                  ALU.add).then_inc(vec_taken[c], 1)

            def stat(layer, c, part):
                if before(layer, part):
                    lb, pb = before(layer, part)
                    dve.wait_ge(x_updated, nth("res", lb, c, pb))
                else:
                    dve.wait_ge(x_in[c], 16)
                n = nth("stat", layer, c, part)
                for t in range(CT):
                    dve.bn_stats(stats[:, c, t], x_tok[:, CT * c + t]).then_inc(stats_done, 1)
                dve.wait_ge(stats_done, CT * n)
                for t in range(CT):
                    dve.bn_aggr(mean_var[:, c, t], stats[:, c, t]).then_inc(aggr_done, 1)
                dve.wait_ge(aggr_done, CT * n)
                dve.tensor_scalar(var_eps[:, c], mean_var[:, c, :, 1], EPS, None, ALU.add).then_inc(var_ready, 1)

            def hat(layer, c, part):
                dve.wait_ge(rstd_ready, nth("rstd", layer, c, part))
                if before(layer, part):
                    lb, pb = before(layer, part)
                    dve.wait_ge(vec_ready[c], vec_use("turn_hat", lb, c, pb) + 1)
                for t in range(CT):
                    last = dve.tensor_scalar(x_hat[:, c, t], x_tok[:, CT * c + t], mean_var[:, c, t, 0:1],
                                             rstd[:, c, t:t + 1], ALU.subtract, ALU.mult)
                last.then_inc(hat_ready, 1)

            def mod(layer, c, part):
                use = vec_use("turn_hat", layer, c, part)
                dve.wait_ge(vec_ready[c], use + 1)
                dve.wait_ge(vec_taken[0], taken("cond", layer, 0, 0))
                if part:
                    dve.wait_ge(lin_ready, lin_use("v", layer, c, 0) + 1)
                elif layer:
                    dve.wait_ge(lin_ready, lin_use("ff1", layer - 1, c, FF[layer - 1] - 1) + 1)
                dve.tensor_tensor(by_seq(x_mod[:, c]), by_seq(vec_bank(c, use)[:, 0:CW]),
                                  ada_of(layer, 3 * part + SCALE, c), ALU.mult).then_inc(vec_taken[c], 1)

            def score_columns(layer, c, g):
                bank = scb[(nth("scores", layer, c, g) - 1) % SCORE_BANKS]
                return bank[:, 0:CW].rearrange("p (n k) -> p n k", k=SEQ)

            def row_maximum(layer, c, g):
                dve.wait_ge(scores_ready, nth("scores", layer, c, g))
                dve.tensor_reduce(row_max[:, c, g], score_columns(layer, c, g), AX_X, ALU.max).then_inc(max_ready, 1)

            def subtract(layer, c, g):
                dve.wait_ge(max_ready, nth("max", layer, c, g))
                dve.tensor_tensor(probs[:, c, g].rearrange("p (n k) -> p n k", k=SEQ), score_columns(layer, c, g),
                                  row_max[:, c, g].unsqueeze(2).broadcast_to([P, CT * HPG, SEQ]),
                                  ALU.subtract).then_inc(scores_taken, 1)

            def turn(layer, c, g):
                dve.wait_ge(probs_ready, nth("exp", layer, c, g))
                if layer:
                    dve.wait_ge(vec_ready[c], vec_use("pv", layer - 1, c, HALVES - 1) + 1)
                dve.transpose(probs_T[:, c, g], probs[:, c, g]).then_inc(probs_turned, 1)

            def norm(layer, c, half):
                use = vec_use("pv", layer, c, half)
                src = vec_bank(c, use)[:, 0:HALF * HEADS * VW].rearrange("p (n w) -> p n w", w=VW)
                dve.wait_ge(vec_ready[c], use + 1)
                dve.reciprocal(sum_inv[:, c, half], src[:, :, CH]).then_inc(inv_ready, 1)
                dve.wait_ge(inv_ready, nth("norm", layer, c, half))
                dst = att[:, c, HALF * P * half:HALF * P * (half + 1)].rearrange("p (n w) -> p n w", w=CH)
                dve.tensor_tensor(dst, src[:, :, 0:CH],
                                  sum_inv[:, c, half].unsqueeze(2).broadcast_to([P, HALF * HEADS, CH]),
                                  ALU.mult).then_inc(vec_taken[c], 1)

            def fold(layer, c, _):
                dve.wait_ge(vec_taken[c], taken("pv", layer, c, HALVES - 1))
                if layer:
                    dve.wait_ge(vec_ready[c], vec_use("proj", layer - 1, c, 0) + 1)
                    dst = att_T[:, c].rearrange("p (l s e) -> p s e l", l=Q_LOW, e=Q_HIGH)
                    dve.transpose(dst, att[:, c]).then_inc(att_turned, 1)
                    dve.wait_ge(att_turned, nth("fold", layer, c))
                    dve.tensor_scalar(att_T[:, c], att_T[:, c], column(B_V), None, ALU.add).then_inc(att_biased, 1)
                else:
                    dve.transpose(att_T[:, c], att[:, c]).then_inc(att_turned, 1)

            def gate(layer, c, part):
                use = vec_use("ff2" if part else "proj", layer, c, 0)
                dve.wait_ge(vec_ready[c], use + 1)
                if before(layer, part):
                    lb, pb = before(layer, part)
                    dve.wait_ge(vec_ready[c], vec_use("turn_gate", lb, c, pb) + 1)
                dve.scalar_tensor_tensor(by_seq(gated[:, c]), by_seq(vec_bank(c, use)[:, 0:CW]),
                                         column((B_FF2 if part else B_O)[layer]),
                                         ada_of(layer, 3 * part + GATE, c), ALU.add,
                                         ALU.mult).then_inc(vec_taken[c], 1)

            def res(layer, c, part):
                use = vec_use("turn_gate", layer, c, part)
                dve.wait_ge(vec_ready[c], use + 1)
                tokens = x_tok[:, CT * c:CT * (c + 1)].rearrange("p t f -> p (t f)")
                dve.tensor_tensor(tokens, tokens, vec_bank(c, use)[:, 0:CW], ALU.add).then_inc(x_updated, 1)

            run({"ada": ada_vectors, "stat": stat, "hat": hat, "mod": mod, "max": row_maximum, "sub": subtract,
                 "turn": turn, "norm": norm, "fold": fold, "gate": gate, "res": res})

        @block.tensor
        def _(pe):
            def free_vec(writer):
                c, use = writer[2], vec_use(*writer)
                if use >= VEC_BANKS:
                    mine = [s for s in SCHEDULE if s[0] in VEC_WRITERS and s[2] == c]
                    held = mine[use - VEC_BANKS]
                    if held[0] == "turn_gate":
                        pe.wait_ge(x_updated, nth("res", *held[1:]))
                    else:
                        pe.wait_ge(vec_taken[c], taken(*held))
                return vec_bank(c, use)

            def free_lin(use):
                if use >= LIN_BANKS:
                    pe.wait_ge(lin_taken, use - LIN_BANKS + 1)
                return lin_bank(use)

            def ada_product(layer, c, _):
                dst = free_vec(("cond", layer, c, 0))
                pe.wait_ge(cond_ready, 1)
                pe.wait_ge(w_first_in[layer], 16)
                for n in range(6):
                    last = pe.matmul(dst[:, BATCH * n:BATCH * (n + 1)], w[layer][:, W_ADA + P * n:W_ADA + P * (n + 1)],
                                     s_cond[:], start=True, stop=True)
                last.then_inc(vec_ready[c], 1)

            def turn_tiles(dst, src, done):
                for t in range(CT):
                    last = pe.transpose(dst[:, P * t:P * (t + 1)], src(t), ident)
                last.then_inc(done, 1)

            def turn_hat(layer, c, part):
                dst = free_vec(("turn_hat", layer, c, part))
                pe.wait_ge(vec_in, 16)
                pe.wait_ge(hat_ready, nth("hat", layer, c, part))
                turn_tiles(dst, lambda t: x_hat[:, c, t], vec_ready[c])

            def feature_major(kind, at):
                def product(layer, c, _):
                    dst = free_lin(lin_use(kind, layer, c, 0))
                    pe.wait_ge(mod_ready, nth("shift", layer, c, 0))
                    pe.wait_ge(w_first_in[layer], 16)
                    pe.matmul(dst[:, 0:CW], w[layer][:, at:at + P], x_mod[:, c], start=True, stop=True).then_inc(lin_ready, 1)
                return product

            def v_product(layer, c, _):
                dst = free_lin(lin_use("v", layer, c, 0))
                pe.wait_ge(mod_ready, nth("shift", layer, c, 0))
                pe.wait_ge(w_first_in[layer], 16)
                for t in range(CT):
                    last = pe.matmul(dst[:, P * t:P * (t + 1)], x_mod[:, c, P * t:P * (t + 1)],
                                     w[layer][:, W_V:W_V + P], start=True, stop=True)
                last.then_inc(lin_ready, 1)

            def scores(layer, c, g):
                n = nth("scores", layer, c, g)
                pe.wait_ge(lin_taken, lin_use("k", layer, c, 0) + 1)
                pe.wait_ge(lin_taken, lin_use("q", layer, c, 0) + 1)
                if n > SCORE_BANKS:
                    pe.wait_ge(scores_taken, n - SCORE_BANKS)
                bank = scb[(n - 1) % SCORE_BANKS]
                rows = slice(QUAD * g, QUAD * (g + 1))
                for t in range(CT):
                    for b in range(SEQ_PER_TILE):
                        seq = slice(P * t + SEQ * b, P * t + SEQ * (b + 1))
                        last = pe.matmul(bank[QUAD * b:QUAD * (b + 1), P * t:P * (t + 1)], qT[rows, c, seq],
                                         kT_mask[rows, c, :, seq], start=True, stop=True)
                last.then_inc(scores_ready, 1)

            def pv(layer, c, half):
                dst = free_vec(("pv", layer, c, half))[:, 0:HALF * HEADS * VW].rearrange(
                    "p (t b h w) -> p t b h w", t=HALF, b=SEQ_PER_TILE, w=VW)
                pe.wait_ge(probs_turned, nth("turn", layer, c, GROUPS - 1))
                pe.wait_ge(lin_taken, lin_use("v", layer, c, 0) + 1)
                for t in range(HALF):
                    for h in range(HPG):
                        for g in range(GROUPS):
                            tile = HALF * half + t
                            q = slice(P * tile + SEQ * h, P * tile + SEQ * (h + 1))
                            last = pe.matmul(dst[QUAD * g:QUAD * (g + 1), t, :, h, :], probs_T[:, c, g, q],
                                             v_own[:, c, tile, HPG * g + h], start=True, stop=True)
                last.then_inc(vec_ready[c], 1)

            def proj(layer, c, _):
                dst = free_vec(("proj", layer, c, 0))
                pe.wait_ge(w_rest_in[layer], 16)
                if layer:
                    pe.wait_ge(att_back[c], 16)
                    src = att_rows[:, c].rearrange("p h (s e) -> p s h e", e=Q_HIGH)
                else:
                    pe.wait_ge(att_turned, nth("fold", layer, c))
                    src = att_T[:, c]
                pe.matmul(dst[:, 0:CW], w[layer][:, W_O:W_O + P], src, start=True, stop=True).then_inc(vec_ready[c], 1)

            def turn_gate(layer, c, part):
                dst = free_vec(("turn_gate", layer, c, part))
                pe.wait_ge(vec_taken[c], taken("ff2" if part else "proj", layer, c, 0))
                turn_tiles(dst, lambda t: gated[:, c, P * t:P * (t + 1)], vec_ready[c])

            def ff1(layer, c, f):
                dst = free_lin(lin_use("ff1", layer, c, f))
                pe.wait_ge(mod_ready, nth("shift", layer, c, 1))
                at = W_FF1 + P * f
                pe.matmul(dst[:, 0:CW], w[layer][:, at:at + P], x_mod[:, c], start=True, stop=True).then_inc(lin_ready, 1)

            def ff2(layer, c, _):
                dst = free_vec(("ff2", layer, c, 0))
                for f in range(FF[layer]):
                    pe.wait_ge(lin_taken, lin_use("ff1", layer, c, f) + 1)
                    at = W_FF2[layer] + P * f
                    last = pe.matmul(dst[:, 0:CW], w[layer][:, at:at + P], hidden[:, c, f],
                                     start=f == 0, stop=f == FF[layer] - 1)
                last.then_inc(vec_ready[c], 1)

            run({"cond": ada_product, "turn_hat": turn_hat, "k": feature_major("k", W_K), "q": feature_major("q", W_Q),
                 "v": v_product, "scores": scores, "pv": pv, "proj": proj, "turn_gate": turn_gate, "ff1": ff1,
                 "ff2": ff2})


def kernel(**inputs):
    import concourse.bacc as bacc
    from concourse.bass_utils import run_bass_kernel_spmd

    a = {name: np.asarray(value) for name, value in inputs.items()}
    l0 = {k[8:]: v for k, v in a.items() if k.startswith("L0_cond_")}
    l1 = {k[8:]: v for k, v in a.items() if k.startswith("L1_cond_")}
    f32 = np.float32

    def columns(v):
        return v.reshape(-1, P).T

    def down(v):
        return v.reshape(-1, P, P).transpose(1, 0, 2).reshape(P, -1)

    masks = (np.arange(P)[:, None] // CH % HPG == np.arange(HPG)[None, :]).astype(f32)
    vectors = np.concatenate(
        [a["cond_1024"].T, masks, np.eye(P, dtype=f32), columns(l0["b_ada"]), columns(l1["bada"]),
         columns(l0["b_proj"]), columns(l1["bo"]), columns(l0["b_mlp1"]), columns(l1["b1"]),
         columns(l0["b_mlp2"]), columns(l1["b2"]), columns(l1["bq"]), columns(l1["bk"]), columns(l1["bv"])], axis=1)
    w_k, w_q, w_v = np.split(l0["w_qkv"], 3, axis=1)
    weights0 = np.concatenate([l0["w_ada"], w_q, w_k, w_v, l0["w_proj"], l0["w_mlp1"], down(l0["w_mlp2"])], axis=1)
    w_o1 = l1["Wo"].reshape(P // CH, CH, P).transpose(1, 0, 2).reshape(P, P)
    weights1 = np.concatenate([l1["Wada"], l1["Wq"], l1["Wk"], l1["Wv"], w_o1, l1["W1"], down(l1["W2"])], axis=1)
    arrays = {
        "x": np.ascontiguousarray(a["x"].reshape(TILES, P, P).transpose(1, 0, 2).reshape(P, -1)),
        "vectors": np.ascontiguousarray(vectors),
        "weights0": np.ascontiguousarray(weights0),
        "weights1": np.ascontiguousarray(weights1),
    }
    nc = bacc.Bacc("TRN2", target_bir_lowering=False, num_devices=1)
    args = [nc.dram_tensor(f"{name}_dram", v.shape, F32, kind="ExternalInput").ap() for name, v in arrays.items()]
    out = nc.dram_tensor("out_dram", (P, TILES * P), F32, kind="ExternalOutput").ap()
    scratch = nc.dram_tensor("scratch_dram", (CHUNKS, HEADS, CH, Q_LOW, CW // Q_LOW), F32, kind="Internal").ap()
    two_blocks(nc, *args, scratch, out)
    r = run_bass_kernel_spmd(nc, [{f"{name}_dram": v for name, v in arrays.items()}], core_ids=[0])
    y = r.results[0]["out_dram"]
    return np.asarray(y).reshape(P, TILES, P).transpose(1, 0, 2).reshape(BATCH, SEQ, P)
```

```python
from contextlib import ExitStack

import numpy as np

import concourse.bass as bass
import concourse.mybir as mybir

F32 = mybir.dt.float32
ALU = mybir.AluOpType
ACT = mybir.ActivationFunctionType
AX_X = mybir.AxisListType.X

P = 128
BATCH, SEQ = 32, 32
HEADS, CH = 16, 8
SEQ_PER_TILE = P // SEQ
TILES = BATCH * SEQ // P
GROUPS = 4
HPG = HEADS // GROUPS
QUAD = 32
EPS = 1e-6
Q_LOW = P // CH
Q_HIGH = SEQ // Q_LOW
VW = CH + 1
FF = (4, 2)
GELU = (ACT.Gelu_apprx_tanh, ACT.Gelu)
SCORE_SCALE = (1.0 / CH, 1.0 / float(np.sqrt(np.float32(CH))))

CHUNKS = 4
CT = TILES // CHUNKS
CW = CT * P
CSEQ = CT * SEQ_PER_TILE
PAIR = 2
PAIRS = GROUPS // PAIR
HALF = 2
HALVES = CT // HALF

COND0 = 0
MASK0 = COND0 + BATCH
GROUP0 = MASK0 + HPG
IDENT0 = GROUP0 + GROUPS
BIAS0 = IDENT0 + P
B_ADA = (BIAS0, BIAS0 + 6)
B_O = (BIAS0 + 12, BIAS0 + 13)
B_FF1 = (BIAS0 + 14, BIAS0 + 18)
B_FF2 = (BIAS0 + 20, BIAS0 + 21)
B_Q, B_K = BIAS0 + 22, BIAS0 + 23
ROW_BV0 = BIAS0 + 24
VEC_COLS = ROW_BV0 + HEADS

W_ADA, W_Q, W_K, W_V = 0, 6 * P, 7 * P, 8 * P
W_O, W_FF1 = 9 * P, 10 * P
W_FF2 = tuple(W_FF1 + f * P for f in FF)
W_COLS = tuple(W_FF2[n] + FF[n] * P for n in range(2))

SHIFT, SCALE, GATE = 0, 1, 2


PLACES = (
    {
        "stat": ((5.0, 5.28, 6.52, 8.33), (27.82, 35.81, 40.31, 44.6)),
        "aggr": ((5.11, 5.59, 7.82, 8.53), (28.36, 35.96, 41.05, 44.71)),
        "cond": ((5.26,), (7.86,)),
        "rstd": ((6.11, 7.35, 8.1, 9.59), (28.46, 36.4, 41.77, 45.83)),
        "hat": ((7.1, 9.33, 8.58, 9.86), (29.47, 36.58, 41.92, 48.97)),
        "ada": ((7.45,), (9.75,)),
        "turn_hat": ((7.48, 10.28, 10.83, 11.26), (30.99, 39.07, 44.31, 49.8)),
        "mod": ((8.2, 11.2, 11.53, 11.54), (32.66, 40.15, 44.32, 50.33)),
        "shift": ((8.38, 12.19, 12.56, 13.81), (32.94, 40.28, 44.81, 51.26)),
        "k": ((8.4, 14.12, 18.07, 24.34),),
        "q": ((9.67, 13.02, 19.59, 21.64),),
        "mask_k": ((11.22, 15.61, 19.42, 26.97),),
        "copy_q": ((12.07, 13.3, 20.79, 23.42),),
        "scores": ((15.58, 16.43, 23.06, 28.51), (16.05, 18.89, 23.16, 29.45)),
        "max": ((15.62, 18.53, 24.67, 28.63), (16.28, 20.21, 26.87, 30.92)),
        "v": ((15.67, 24.56, 30.23, 30.75),),
        "sub": ((16.01, 20.4, 24.72, 30.61), (16.63, 20.45, 27.94, 32.59)),
        "copy_v": ((16.5, 27.38, 32.37, 32.52),),
        "exp": ((16.58, 22.69, 25.25, 30.9), (17.97, 24.52, 28.84, 34.01)),
        "turn": ((17.55, 23.56, 26.06, 32.97), (18.94, 24.98, 29.48, 34.65)),
        "pv": ((21.17, 29.27, 32.47, 35.87),),
        "inv": ((22.83, 30.38, 33.41, 36.55),),
        "norm": ((23.26, 30.73, 35.72, 37.1),),
        "fold": ((23.68, 31.9, 36.38, 37.54),),
        "proj": ((24.27, 32.34, 37.52, 38.03),),
        "gate": ((25.83, 33.02, 38.16, 39.22), (41.49, 46.18, 54.77, 60.92)),
        "turn_gate": ((26.02, 33.13, 38.49, 43.53), (42.03, 46.49, 55.18, 61.66)),
        "res": ((26.5, 35.5, 39.86, 44.21), (42.22, 47.22, 55.33, 61.68)),
        "ff1": ((32.99, 41.1, 45.8, 52.49), (33.55, 42.0, 46.95, 54.03), (36.54, 42.26, 47.4, 54.18),
                (37.24, 43.42, 50.43, 55.24)),
        "gelu": ((35.3, 41.88, 46.26, 54.34), (36.65, 42.99, 47.03, 54.72), (38.36, 43.24, 47.59, 55.26),
                 (39.29, 44.69, 51.04, 57.32)),
        "ff2": ((39.7, 45.04, 52.94, 60.44),),
    },
    {
        "stat": ((43.01, 48.32, 55.73, 63.17), (73.7, 86.14, 84.66, 88.77)),
        "aggr": ((43.99, 48.34, 56.08, 64.42), (80.56, 86.16, 85.8, 89.55)),
        "cond": ((11.3,), (13.2,)),
        "rstd": ((44.4, 49.73, 56.85, 64.54), (81.41, 87.51, 86.38, 90.87)),
        "hat": ((44.76, 50.32, 57.33, 65.88), (82.01, 87.99, 87.31, 91.02)),
        "ada": ((11.97,), (14.04,)),
        "turn_hat": ((46.23, 50.47, 58.71, 66.14), (83.2, 88.11, 88.01, 91.96)),
        "mod": ((46.51, 51.98, 59.05, 66.7), (83.59, 90.32, 88.05, 92.03)),
        "shift": ((46.54, 52.47, 61.2, 68.06), (84.69, 92.34, 88.32, 94.1)),
        "k": ((47.6, 58.04, 62.0, 68.54),),
        "q": ((51.38, 55.86, 61.39, 68.82),),
        "mask_k": ((48.55, 59.71, 66.26, 69.58),),
        "copy_q": ((52.7, 57.34, 63.09, 70.48),),
        "scores": ((57.8, 62.21, 67.82, 73.12), (58.59, 64.49, 70.5, 74.58)),
        "max": ((58.93, 64.17, 68.37, 74.2), (59.67, 65.47, 70.75, 76.47)),
        "v": ((49.97, 74.68, 65.28, 71.69),),
        "sub": ((59.04, 65.08, 70.19, 77.08), (60.04, 66.04, 72.14, 77.38)),
        "copy_v": ((49.99, 74.72, 68.1, 74.29),),
        "exp": ((59.38, 67.17, 72.74, 77.36), (62.71, 68.65, 73.81, 77.64)),
        "turn": ((62.73, 69.95, 73.33, 78.2), (63.0, 70.6, 75.98, 78.51)),
        "pv": ((64.75, 76.22, 76.04, 78.52),),
        "inv": ((67.64, 79.12, 77.83, 80.78),),
        "norm": ((67.95, 79.83, 78.57, 81.09),),
        "fold": ((68.84, 80.57, 79.27, 83.22),),
        "proj": ((70.82, 82.52, 81.36, 86.63),),
        "gate": ((71.18, 83.62, 83.58, 86.69), (89.69, 96.03, 92.08, 97.27)),
        "turn_gate": ((72.59, 84.04, 83.85, 87.36), (90.75, 97.2, 93.55, 98.22)),
        "res": ((72.91, 85.13, 84.24, 88.4), (91.26, 97.51, 94.26, 98.57)),
        "ff1": ((84.73, 92.79, 89.81, 94.25), (85.77, 93.18, 90.23, 94.47)),
        "gelu": ((85.26, 93.59, 91.11, 94.84), (88.26, 94.46, 91.16, 95.56)),
        "ff2": ((88.27, 95.05, 91.57, 96.57),),
        "turn_rows": ((69.45, 81.12, 80.17, 84.03),),
        "rows": ((70.23, 81.63, 80.83, 84.3),),
    },
)


def schedule():
    return [step for _, step in sorted((at, (kind, layer, chunk, part))
                                       for layer in range(2) for kind, parts in PLACES[layer].items()
                                       for part, places in enumerate(parts)
                                       for chunk, at in enumerate(places))]


LIN_READER = {"k": "mask_k", "q": "copy_q", "v": "copy_v", "ff1": "gelu"}
SCHEDULE = schedule()


def nth(kind, layer, chunk, part=0):
    at = SCHEDULE.index((kind, layer, chunk, part))
    return sum(s[0] == kind for s in SCHEDULE[:at + 1])


GPSIMD_NORMS = ((0, 1),)


def norm_engine(layer, part):
    return int((layer, part) in GPSIMD_NORMS)


def nth_hat(layer, chunk, part):
    at = SCHEDULE.index(("hat", layer, chunk, part))
    return sum(s[0] == "hat" and norm_engine(s[1], s[3]) == norm_engine(layer, part) for s in SCHEDULE[:at + 1])


VEC_WRITERS = ("cond", "turn_hat", "pv", "turn_rows", "proj", "turn_gate", "ff2")

def lin_use(*writer):
    return sum(s[0] in LIN_READER for s in SCHEDULE[:SCHEDULE.index(writer)])


def vec_use(*writer):
    return sum(s[0] in VEC_WRITERS and s[2] == writer[2] for s in SCHEDULE[:SCHEDULE.index(writer)])


def taken(*writer):
    return sum(s[0] in VEC_WRITERS and s[0] != "turn_gate" and s[2] == writer[2]
               for s in SCHEDULE[:SCHEDULE.index(writer) + 1])


def before(layer, part):
    if part:
        return layer, 0
    return (layer - 1, 1) if layer else None


BUSY = (11, 2, 4)
LIN_BANKS, SCORE_BANKS = 2, 2
VEC_BANKS = 4 // CHUNKS


def two_blocks(nc, x, vectors, weights0, weights1, out):
    with ExitStack() as ctx:
        def sb(name, shape):
            return ctx.enter_context(nc.sbuf_tensor(name, shape, F32))

        def bank(name):
            return ctx.enter_context(nc.psum_tensor(name, [P, 512], F32))

        def sem(name):
            return ctx.enter_context(nc.semaphore(name))

        x_tok = sb("x_tok", [P, TILES, P])
        vec = sb("vec", [P, VEC_COLS])
        w = [sb("w0", [P, W_COLS[0]]), sb("w1", [P, W_COLS[1]])]
        exp_of_zero = sb("exp_of_zero", [P, 1])
        e_cond = sb("e_cond", [P, BATCH])
        s_cond = sb("s_cond", [P, BATCH])
        ada = sb("ada", [P, 2, 6, BATCH])
        b_ada1 = sb("b_ada1", [P, 2, 6])
        bk_mask = sb("bk_mask", [P, HPG])
        bq_mask = sb("bq_mask", [P, GROUPS])
        half_neg = sb("half_neg", [P, CT])
        idle = sb("idle", [P, P])
        stats = sb("stats", [P, CHUNKS, CT, 6])
        mean_var = sb("mean_var", [P, CHUNKS, CT, 2])
        var_eps = sb("var_eps", [P, CHUNKS, CT])
        rstd = sb("rstd", [P, CHUNKS, CT])
        mean_neg = sb("mean_neg", [P, CHUNKS, CT])
        mean_rstd = sb("mean_rstd", [P, CHUNKS, CT])
        x_hat = sb("x_hat", [P, CHUNKS, CT, P])
        x_mod = sb("x_mod", [P, CHUNKS, CW])
        qT_group = sb("qT_group", [P, CHUNKS, GROUPS, CW])
        kT_mask = sb("kT_mask", [P, CHUNKS, HPG, CW])
        v_own = sb("v_own", [P, CHUNKS, CT, HEADS, SEQ_PER_TILE, VW])
        row_max = sb("row_max", [P, CHUNKS, PAIRS, PAIR * CT * HPG])
        probs = sb("probs", [P, CHUNKS, PAIRS, PAIR * CW])
        probs_T = sb("probs_T", [P, CHUNKS, PAIRS, PAIR * CW])
        sum_inv = sb("sum_inv", [P, CHUNKS, HALVES, HALF * HEADS])
        att = sb("att", [P, CHUNKS, CW])
        att_T = sb("att_T", [P, CHUNKS, CW])
        att_rows = sb("att_rows", [P, CHUNKS, CW])
        gated = sb("gated", [P, CHUNKS, CW])
        hidden = sb("hidden", [P, CHUNKS, max(FF), CW])

        lin = [bank(f"lin{n}") for n in range(LIN_BANKS)]
        vecb = [bank(f"vecb{n}") for n in range(CHUNKS * VEC_BANKS)]
        scb = [bank(f"scb{n}") for n in range(SCORE_BANKS)]

        x_in = [sem(f"x_in{c}") for c in range(CHUNKS)]
        vec_in = sem("vec_in")
        w_ada_in = [sem("w0_ada_in"), sem("w1_ada_in")]
        w_qkv_in = [sem("w0_qkv_in"), sem("w1_qkv_in")]
        w_rest_in = [sem("w0_rest_in"), sem("w1_rest_in")]
        idle_ready = sem("idle_ready")
        exp_cond = sem("exp_cond")
        cond_step = sem("cond_step")
        cond_ready = sem("cond_ready")
        consts_ready = sem("consts_ready")
        exponent_ready = sem("exponent_ready")
        v_zeroed = sem("v_zeroed")
        v_ones = sem("v_ones")
        stats_done = sem("stats_done")
        aggr_done = sem("aggr_done")
        var_ready = sem("var_ready")
        rstd_ready = sem("rstd_ready")
        neg_ready = sem("neg_ready")
        mean_ready = sem("mean_ready")
        hat_ready = [sem("hat0_ready"), sem("hat1_ready")]
        mod_ready = sem("mod_ready")
        lin_ready = sem("lin_ready")
        lin_taken = sem("lin_taken")
        vec_ready = [sem(f"vec_ready{c}") for c in range(CHUNKS)]
        vec_taken = [sem(f"vec_taken{c}") for c in range(CHUNKS)]
        scores_ready = sem("scores_ready")
        scores_taken = sem("scores_taken")
        max_ready = sem("max_ready")
        probs_ready = sem("probs_ready")
        probs_turned = sem("probs_turned")
        inv_ready = sem("inv_ready")
        att_turned = sem("att_turned")
        x_updated = sem("x_updated")
        out_done = sem("out_done")

        ident = vec[:, IDENT0:IDENT0 + P]

        def column(n):
            return vec[:, n:n + 1]

        def lin_bank(use):
            return lin[use % LIN_BANKS]

        def vec_bank(chunk, use):
            return vecb[VEC_BANKS * chunk + use % VEC_BANKS]

        def by_seq(ap):
            return ap.rearrange("p (s k) -> p s k", k=SEQ)

        def ada_of(layer, which, chunk):
            v = ada[:, layer, which, CSEQ * chunk:CSEQ * (chunk + 1)]
            return v.unsqueeze(2).broadcast_to([P, CSEQ, SEQ])

        def run(parts):
            for kind, layer, chunk, part in SCHEDULE:
                if kind in parts:
                    parts[kind](layer, chunk, part)

        block = ctx.enter_context(nc.Block())

        @block.sync
        def _(sp):
            def chunks_in(first, last):
                for c in range(first, last):
                    sp.dma_start(x_tok[:, CT * c:CT * (c + 1), :],
                                 x[:, CW * c:CW * (c + 1)].rearrange("p (t f) -> p t f", f=P)).then_inc(x_in[c], 16)

            chunks_in(0, 1)
            sp.dma_start(w[0][:, 0:W_Q], weights0[:, 0:W_Q]).then_inc(w_ada_in[0], 16)
            chunks_in(1, 2)
            sp.dma_start(w[0][:, W_Q:W_O], weights0[:, W_Q:W_O]).then_inc(w_qkv_in[0], 16)
            chunks_in(2, CHUNKS)
            sp.dma_start(w[0][:, W_O:], weights0[:, W_O:]).then_inc(w_rest_in[0], 16)
            sp.dma_start(w[1][:, 0:W_Q], weights1[:, 0:W_Q]).then_inc(w_ada_in[1], 16)
            sp.dma_start(w[1][:, W_Q:W_O], weights1[:, W_Q:W_O]).then_inc(w_qkv_in[1], 16)
            sp.dma_start(w[1][:, W_O:], weights1[:, W_O:]).then_inc(w_rest_in[1], 16)
            for c in sorted(range(CHUNKS), key=lambda c: nth("res", 1, c, 1)):
                sp.wait_ge(x_updated, nth("res", 1, c, 1))
                sp.dma_start(out[:, CW * c:CW * (c + 1)],
                             x_tok[:, CT * c:CT * (c + 1), :].rearrange("p t f -> p (t f)")).then_inc(out_done, 16)
            sp.wait_ge(out_done, 16 * CHUNKS)

        @block.gpsimd
        def _(pool):
            pool.memset(half_neg[:], -0.5).then_inc(exponent_ready, 1)
            for c in range(CHUNKS // 2):
                pool.memset(v_own[:, c], 0.0).then_inc(v_zeroed, 1)
            pool.wait_ge(v_zeroed, CHUNKS)
            for b in range(SEQ_PER_TILE):
                rows = slice(QUAD * b, QUAD * (b + 1))
                pool.memset(v_own[rows, :, :, :, b, CH:VW], 1.0).then_inc(v_ones, 1)
                pool.wait_ge(v_ones, b + 1)

            def rstd_power(layer, c, part):
                pool.wait_ge(aggr_done, CT * nth("aggr", layer, c, part))
                pool.wait_ge(exponent_ready, 1)
                if before(layer, part):
                    lb, pb = before(layer, part)
                    pool.wait_ge(hat_ready[norm_engine(lb, pb)], nth_hat(lb, c, pb))
                pool.tensor_scalar(var_eps[:, c], mean_var[:, c, :, 1], EPS, None, ALU.add).then_inc(var_ready, 1)
                if (layer, part) in GPSIMD_NORMS:
                    pool.tensor_scalar(mean_neg[:, c], mean_var[:, c, :, 0], -1.0, None,
                                       ALU.mult).then_inc(neg_ready, 1)
                pool.wait_ge(var_ready, nth("rstd", layer, c, part))
                pool.tensor_tensor(rstd[:, c], var_eps[:, c], half_neg[:], ALU.pow).then_inc(rstd_ready, 1)

            def hat(layer, c, part):
                if (layer, part) not in GPSIMD_NORMS:
                    return
                n = nth_hat(layer, c, part)
                pool.wait_ge(rstd_ready, nth("rstd", layer, c, part))
                pool.wait_ge(neg_ready, n)
                if before(layer, part):
                    lb, pb = before(layer, part)
                    pool.wait_ge(vec_ready[c], vec_use("turn_hat", lb, c, pb) + 1)
                pool.tensor_tensor(mean_rstd[:, c], mean_neg[:, c], rstd[:, c], ALU.mult).then_inc(mean_ready, 1)
                pool.wait_ge(mean_ready, n)
                for t in range(CT):
                    last = pool.tensor_scalar(x_hat[:, c, t], x_tok[:, CT * c + t], rstd[:, c, t:t + 1],
                                              mean_rstd[:, c, t:t + 1], ALU.mult, ALU.add)
                last.then_inc(hat_ready[1], 1)

            def shift(layer, c, part):
                pool.wait_ge(vec_taken[c], taken("turn_hat", layer, c, part))
                pool.tensor_tensor(by_seq(x_mod[:, c]), by_seq(x_mod[:, c]), ada_of(layer, 3 * part + SHIFT, c),
                                   ALU.add).then_inc(mod_ready, 1)

            run({"rstd": rstd_power, "hat": hat, "shift": shift})

        @block.scalar
        def _(act):
            act.dma_start(vec[:], vectors).then_inc(vec_in, 16)
            act.wait_ge(idle_ready, 1)
            act.activation(exp_of_zero[:], idle[:, 0:1], ACT.Exp)
            act.wait_ge(vec_in, 16)
            act.activation(e_cond[:], vec[:, COND0:COND0 + BATCH], ACT.Exp, scale=-1.0).then_inc(exp_cond, 1)
            act.wait_ge(consts_ready, 2)

            def mask_k(layer, c, _):
                use = lin_use("k", layer, c, 0)
                act.wait_ge(lin_ready, use + 1)
                if layer:
                    act.wait_ge(scores_ready, nth("scores", layer - 1, c, PAIRS - 1))
                for h in range(HPG):
                    last = act.activation(kT_mask[:, c, h], lin_bank(use)[:, 0:CW], ACT.Identity,
                                          scale=column(MASK0 + h), bias=bk_mask[:, h:h + 1] if layer else 0.0)
                last.then_inc(lin_taken, 1)

            def copy_q(layer, c, _):
                use = lin_use("q", layer, c, 0)
                act.wait_ge(lin_ready, use + 1)
                if layer:
                    act.wait_ge(scores_ready, nth("scores", layer - 1, c, PAIRS - 1))
                for g in range(GROUPS):
                    last = act.activation(qT_group[:, c, g], lin_bank(use)[:, 0:CW], ACT.Identity,
                                          scale=column(GROUP0 + g), bias=bq_mask[:, g:g + 1] if layer else 0.0)
                last.then_inc(lin_taken, 1)

            def copy_v(layer, c, _):
                use = lin_use("v", layer, c, 0)
                act.wait_ge(lin_ready, use + 1)
                if layer:
                    act.wait_ge(vec_ready[c], vec_use("pv", layer - 1, c, HALVES - 1) + 1)
                else:
                    act.wait_ge(v_ones, SEQ_PER_TILE)
                for b in range(SEQ_PER_TILE):
                    rows = slice(QUAD * b, QUAD * (b + 1))
                    last = act.activation(v_own[rows, c, :, :, b, 0:CH].rearrange("p t h c -> p (t h) c"),
                                          lin_bank(use)[rows, 0:CW].rearrange("p (n c) -> p n c", c=CH),
                                          ACT.Identity)
                last.then_inc(lin_taken, 1)

            def exp(layer, c, pair):
                act.wait_ge(scores_taken, nth("sub", layer, c, pair))
                act.activation(probs[:, c, pair], probs[:, c, pair], ACT.Exp,
                               scale=SCORE_SCALE[layer]).then_inc(probs_ready, 1)

            def gelu(layer, c, f):
                use = lin_use("ff1", layer, c, f)
                act.wait_ge(lin_ready, use + 1)
                if layer:
                    act.wait_ge(vec_ready[c], vec_use("ff2", layer - 1, c, 0) + 1)
                act.activation(hidden[:, c, f], lin_bank(use)[:, 0:CW], GELU[layer],
                               bias=column(B_FF1[layer] + f)).then_inc(lin_taken, 1)

            run({"mask_k": mask_k, "copy_q": copy_q, "copy_v": copy_v, "exp": exp,
                 "gelu": gelu})

        @block.vector
        def _(dve):
            dve.memset(idle[:], 0.0).then_inc(idle_ready, 1)
            for c in range(CHUNKS // 2, CHUNKS):
                dve.memset(v_own[:, c], 0.0).then_inc(v_zeroed, 1)
            dve.wait_ge(vec_in, 16)
            dve.tensor_scalar(bk_mask[:], vec[:, MASK0:MASK0 + HPG], column(B_K),
                              None, ALU.mult).then_inc(consts_ready, 1)
            dve.tensor_scalar(bq_mask[:], vec[:, GROUP0:GROUP0 + GROUPS], column(B_Q),
                              None, ALU.mult).then_inc(consts_ready, 1)
            dve.tensor_copy(b_ada1[:].rearrange("p l n -> p (l n)"), vec[:, BIAS0:BIAS0 + 12]).then_inc(consts_ready, 1)
            dve.wait_ge(consts_ready, 3)
            dve.tensor_scalar(b_ada1[:, :, SCALE::3], b_ada1[:, :, SCALE::3], 1.0,
                              None, ALU.add).then_inc(consts_ready, 1)
            dve.wait_ge(exp_cond, 1)
            dve.tensor_scalar(e_cond[:], e_cond[:], 1.0, None, ALU.add).then_inc(cond_step, 1)
            dve.wait_ge(cond_step, 1)
            dve.reciprocal(e_cond[:], e_cond[:]).then_inc(cond_step, 1)
            dve.wait_ge(cond_step, 2)
            dve.tensor_tensor(s_cond[:], e_cond[:], vec[:, COND0:COND0 + BATCH], ALU.mult).then_inc(cond_ready, 1)
            dve.wait_ge(consts_ready, 4)

            def ada_vectors(layer, c, part):
                use = vec_use("cond", layer, c, part)
                which = slice(3 * part, 3 * part + 3)
                dve.wait_ge(vec_ready[c], use + 1)
                dve.tensor_tensor(ada[:, layer, which],
                                  vec_bank(c, use)[:, 0:3 * BATCH].rearrange("p (n b) -> p n b", b=BATCH),
                                  b_ada1[:, layer, which].unsqueeze(2).broadcast_to([P, 3, BATCH]),
                                  ALU.add).then_inc(vec_taken[c], 1)

            def stat(layer, c, part):
                if before(layer, part):
                    lb, pb = before(layer, part)
                    dve.wait_ge(x_updated, nth("res", lb, c, pb))
                else:
                    dve.wait_ge(x_in[c], 16)
                for t in range(CT):
                    dve.bn_stats(stats[:, c, t], x_tok[:, CT * c + t]).then_inc(stats_done, 1)

            def aggregate(layer, c, part):
                dve.wait_ge(stats_done, CT * nth("stat", layer, c, part))
                for t in range(CT):
                    dve.bn_aggr(mean_var[:, c, t], stats[:, c, t]).then_inc(aggr_done, 1)

            def hat(layer, c, part):
                if (layer, part) in GPSIMD_NORMS:
                    return
                dve.wait_ge(rstd_ready, nth("rstd", layer, c, part))
                if before(layer, part):
                    lb, pb = before(layer, part)
                    dve.wait_ge(vec_ready[c], vec_use("turn_hat", lb, c, pb) + 1)
                for t in range(CT):
                    last = dve.tensor_scalar(x_hat[:, c, t], x_tok[:, CT * c + t], mean_var[:, c, t, 0:1],
                                             rstd[:, c, t:t + 1], ALU.subtract, ALU.mult)
                last.then_inc(hat_ready[0], 1)

            def mod(layer, c, part):
                use = vec_use("turn_hat", layer, c, part)
                dve.wait_ge(vec_ready[c], use + 1)
                dve.wait_ge(vec_taken[0], taken("cond", layer, 0, part))
                if part:
                    dve.wait_ge(lin_ready, lin_use("v", layer, c, 0) + 1)
                elif layer:
                    dve.wait_ge(lin_ready, lin_use("ff1", layer - 1, c, FF[layer - 1] - 1) + 1)
                dve.tensor_tensor(by_seq(x_mod[:, c]), by_seq(vec_bank(c, use)[:, 0:CW]),
                                  ada_of(layer, 3 * part + SCALE, c), ALU.mult).then_inc(vec_taken[c], 1)

            def score_columns(layer, c, pair):
                bank = scb[(nth("scores", layer, c, pair) - 1) % SCORE_BANKS]
                return bank[:, 0:PAIR * CW].rearrange("p (n k) -> p n k", k=SEQ)

            def row_maximum(layer, c, pair):
                dve.wait_ge(scores_ready, nth("scores", layer, c, pair))
                dve.tensor_reduce(row_max[:, c, pair], score_columns(layer, c, pair), AX_X,
                                  ALU.max).then_inc(max_ready, 1)

            def subtract(layer, c, pair):
                dve.wait_ge(max_ready, nth("max", layer, c, pair))
                dve.tensor_tensor(probs[:, c, pair].rearrange("p (n k) -> p n k", k=SEQ), score_columns(layer, c, pair),
                                  row_max[:, c, pair].unsqueeze(2).broadcast_to([P, PAIR * CT * HPG, SEQ]),
                                  ALU.subtract).then_inc(scores_taken, 1)

            def turn(layer, c, pair):
                dve.wait_ge(probs_ready, nth("exp", layer, c, pair))
                if layer:
                    dve.wait_ge(vec_ready[c], vec_use("pv", layer - 1, c, HALVES - 1) + 1)
                dve.transpose(probs_T[:, c, pair], probs[:, c, pair]).then_inc(probs_turned, 1)

            def pv_columns(layer, c, half):
                src = vec_bank(c, vec_use("pv", layer, c, half))[:, 0:HALF * HEADS * VW]
                return src.rearrange("p (n w) -> p n w", w=VW)

            def invert(layer, c, half):
                dve.wait_ge(vec_ready[c], vec_use("pv", layer, c, half) + 1)
                dve.reciprocal(sum_inv[:, c, half], pv_columns(layer, c, half)[:, :, CH]).then_inc(inv_ready, 1)

            def norm(layer, c, half):
                dve.wait_ge(inv_ready, nth("inv", layer, c, half))
                dst = att[:, c, HALF * P * half:HALF * P * (half + 1)]
                dst = dst.rearrange("p (w n) -> p n w", w=CH) if layer else dst.rearrange("p (n w) -> p n w", w=CH)
                dve.tensor_tensor(dst, pv_columns(layer, c, half)[:, :, 0:CH],
                                  sum_inv[:, c, half].unsqueeze(2).broadcast_to([P, HALF * HEADS, CH]),
                                  ALU.mult).then_inc(vec_taken[c], 1)

            def fold(layer, c, _):
                dve.wait_ge(vec_taken[c], taken("pv", layer, c, HALVES - 1))
                if layer:
                    dve.wait_ge(vec_ready[c], vec_use("proj", layer - 1, c, 0) + 1)
                dst = att_T[:, c]
                if layer:
                    dst = dst.rearrange("p (e c l) -> p c e l", c=CH, e=Q_HIGH)
                dve.transpose(dst, att[:, c]).then_inc(att_turned, 1)

            def rows(layer, c, _):
                use = vec_use("turn_rows", layer, c, 0)
                dve.wait_ge(vec_ready[c], use + 1)
                bias = vec[:, ROW_BV0:ROW_BV0 + HEADS].rearrange("p (g h) -> p g h", g=GROUPS)
                for e in range(Q_HIGH):
                    src = vec_bank(c, use)[:, P * e:P * (e + 1)].rearrange("p (g s h) -> p g s h", g=GROUPS, h=HPG)
                    dst = att_rows[:, c].rearrange("p (s g h e) -> p g s h e", g=GROUPS, h=HPG, e=Q_HIGH)[:, :, :, :, e]
                    last = dve.tensor_tensor(dst, src, bias.unsqueeze(2).broadcast_to([P, GROUPS, CSEQ, HPG]), ALU.add)
                last.then_inc(vec_taken[c], 1)

            def gate(layer, c, part):
                use = vec_use("ff2" if part else "proj", layer, c, 0)
                dve.wait_ge(vec_ready[c], use + 1)
                if before(layer, part):
                    lb, pb = before(layer, part)
                    dve.wait_ge(vec_ready[c], vec_use("turn_gate", lb, c, pb) + 1)
                dve.scalar_tensor_tensor(by_seq(gated[:, c]), by_seq(vec_bank(c, use)[:, 0:CW]),
                                         column((B_FF2 if part else B_O)[layer]),
                                         ada_of(layer, 3 * part + GATE, c), ALU.add,
                                         ALU.mult).then_inc(vec_taken[c], 1)

            def res(layer, c, part):
                use = vec_use("turn_gate", layer, c, part)
                dve.wait_ge(vec_ready[c], use + 1)
                tokens = x_tok[:, CT * c:CT * (c + 1)].rearrange("p t f -> p (t f)")
                dve.tensor_tensor(tokens, tokens, vec_bank(c, use)[:, 0:CW], ALU.add).then_inc(x_updated, 1)

            run({"ada": ada_vectors, "stat": stat, "aggr": aggregate, "hat": hat, "mod": mod,
                 "max": row_maximum, "sub": subtract, "inv": invert,
                 "turn": turn, "norm": norm, "fold": fold, "rows": rows, "gate": gate, "res": res})

        @block.tensor
        def _(pe):
            def free_vec(writer):
                c, use = writer[2], vec_use(*writer)
                if use >= VEC_BANKS:
                    mine = [s for s in SCHEDULE if s[0] in VEC_WRITERS and s[2] == c]
                    held = mine[use - VEC_BANKS]
                    if held[0] == "turn_gate":
                        pe.wait_ge(x_updated, nth("res", *held[1:]))
                    else:
                        pe.wait_ge(vec_taken[c], taken(*held))
                return vec_bank(c, use)

            def free_lin(use):
                if use >= LIN_BANKS:
                    pe.wait_ge(lin_taken, use - LIN_BANKS + 1)
                return lin_bank(use)

            def keep_busy(products):
                pe.wait_ge(idle_ready, 1)
                for _ in range(products):
                    pe.matmul(scb[0][:, 0:P], idle[:], idle[:], start=True, stop=True)

            def ada_product(layer, c, part):
                dst = free_vec(("cond", layer, c, part))
                if not (layer or part):
                    keep_busy(BUSY[0])
                pe.wait_ge(cond_ready, 1)
                pe.wait_ge(w_ada_in[layer], 16)
                for n in range(3):
                    at = W_ADA + P * (3 * part + n)
                    last = pe.matmul(dst[:, BATCH * n:BATCH * (n + 1)], w[layer][:, at:at + P], s_cond[:],
                                     start=True, stop=True)
                last.then_inc(vec_ready[c], 1)
                if not (layer or part):
                    keep_busy(BUSY[1])

            def turn_tiles(dst, src, done):
                for t in range(CT):
                    last = pe.transpose(dst[:, P * t:P * (t + 1)], src(t), ident)
                last.then_inc(done, 1)

            def turn_hat(layer, c, part):
                dst = free_vec(("turn_hat", layer, c, part))
                pe.wait_ge(vec_in, 16)
                pe.wait_ge(hat_ready[norm_engine(layer, part)], nth_hat(layer, c, part))
                turn_tiles(dst, lambda t: x_hat[:, c, t], vec_ready[c])
                if (layer, c, part) == (0, 0, 0):
                    keep_busy(BUSY[2])

            def feature_major(kind, at):
                def product(layer, c, _):
                    dst = free_lin(lin_use(kind, layer, c, 0))
                    pe.wait_ge(mod_ready, nth("shift", layer, c, 0))
                    pe.wait_ge(w_qkv_in[layer], 16)
                    pe.matmul(dst[:, 0:CW], w[layer][:, at:at + P], x_mod[:, c],
                              start=True, stop=True).then_inc(lin_ready, 1)
                return product

            def v_product(layer, c, _):
                dst = free_lin(lin_use("v", layer, c, 0))
                pe.wait_ge(mod_ready, nth("shift", layer, c, 0))
                pe.wait_ge(w_qkv_in[layer], 16)
                for t in range(CT):
                    last = pe.matmul(dst[:, P * t:P * (t + 1)], x_mod[:, c, P * t:P * (t + 1)],
                                     w[layer][:, W_V:W_V + P], start=True, stop=True)
                last.then_inc(lin_ready, 1)

            def scores(layer, c, pair):
                n = nth("scores", layer, c, pair)
                pe.wait_ge(lin_taken, lin_use("k", layer, c, 0) + 1)
                pe.wait_ge(lin_taken, lin_use("q", layer, c, 0) + 1)
                if n > SCORE_BANKS:
                    pe.wait_ge(scores_taken, n - SCORE_BANKS)
                bank = scb[(n - 1) % SCORE_BANKS]
                for i in range(PAIR):
                    for t in range(CT):
                        cols = slice(CW * i + P * t, CW * i + P * (t + 1))
                        for b in range(SEQ_PER_TILE):
                            seq = slice(P * t + SEQ * b, P * t + SEQ * (b + 1))
                            last = pe.matmul(bank[QUAD * b:QUAD * (b + 1), cols], qT_group[:, c, PAIR * pair + i, seq],
                                             kT_mask[:, c, :, seq], start=True, stop=True)
                last.then_inc(scores_ready, 1)

            def pv(layer, c, half):
                dst = free_vec(("pv", layer, c, half))[:, 0:HALF * HEADS * VW].rearrange(
                    "p (t b h w) -> p t b h w", t=HALF, b=SEQ_PER_TILE, w=VW)
                pe.wait_ge(probs_turned, nth("turn", layer, c, PAIRS - 1))
                pe.wait_ge(lin_taken, lin_use("v", layer, c, 0) + 1)
                for t in range(HALF):
                    for h in range(HPG):
                        for g in range(GROUPS):
                            tile = HALF * half + t
                            first = CW * (g % PAIR) + P * tile + SEQ * h
                            q = slice(first, first + SEQ)
                            last = pe.matmul(dst[QUAD * g:QUAD * (g + 1), t, :, h, :], probs_T[:, c, g // PAIR, q],
                                             v_own[:, c, tile, HPG * g + h], start=True, stop=True)
                last.then_inc(vec_ready[c], 1)

            def turn_rows(layer, c, _):
                dst = free_vec(("turn_rows", layer, c, 0))
                pe.wait_ge(att_turned, nth("fold", layer, c))
                for e in range(Q_HIGH):
                    last = pe.transpose(dst[:, P * e:P * (e + 1)], att_T[:, c, P * e:P * (e + 1)], ident)
                last.then_inc(vec_ready[c], 1)

            def proj(layer, c, _):
                dst = free_vec(("proj", layer, c, 0))
                pe.wait_ge(w_rest_in[layer], 16)
                if layer:
                    pe.wait_ge(vec_taken[c], taken("turn_rows", layer, c, 0))
                    src = att_rows[:, c]
                else:
                    pe.wait_ge(att_turned, nth("fold", layer, c))
                    src = att_T[:, c]
                pe.matmul(dst[:, 0:CW], w[layer][:, W_O:W_O + P], src, start=True, stop=True).then_inc(vec_ready[c], 1)

            def turn_gate(layer, c, part):
                dst = free_vec(("turn_gate", layer, c, part))
                pe.wait_ge(vec_taken[c], taken("ff2" if part else "proj", layer, c, 0))
                turn_tiles(dst, lambda t: gated[:, c, P * t:P * (t + 1)], vec_ready[c])

            def ff1(layer, c, f):
                dst = free_lin(lin_use("ff1", layer, c, f))
                pe.wait_ge(mod_ready, nth("shift", layer, c, 1))
                at = W_FF1 + P * f
                pe.matmul(dst[:, 0:CW], w[layer][:, at:at + P], x_mod[:, c],
                              start=True, stop=True).then_inc(lin_ready, 1)

            def ff2(layer, c, _):
                dst = free_vec(("ff2", layer, c, 0))
                for f in range(FF[layer]):
                    pe.wait_ge(lin_taken, lin_use("ff1", layer, c, f) + 1)
                    at = W_FF2[layer] + P * f
                    last = pe.matmul(dst[:, 0:CW], w[layer][:, at:at + P], hidden[:, c, f],
                                     start=f == 0, stop=f == FF[layer] - 1)
                last.then_inc(vec_ready[c], 1)

            run({"cond": ada_product, "turn_hat": turn_hat, "k": feature_major("k", W_K),
                 "q": feature_major("q", W_Q), "v": v_product, "scores": scores, "pv": pv,
                 "turn_rows": turn_rows, "proj": proj, "turn_gate": turn_gate, "ff1": ff1, "ff2": ff2})


def kernel(**inputs):
    import concourse.bacc as bacc
    from concourse.bass_utils import run_bass_kernel_spmd

    a = {name: np.asarray(value) for name, value in inputs.items()}
    l0 = {k[8:]: v for k, v in a.items() if k.startswith("L0_cond_")}
    l1 = {k[8:]: v for k, v in a.items() if k.startswith("L1_cond_")}
    f32 = np.float32

    def columns(v):
        return v.reshape(-1, P).T

    def down(v):
        return v.reshape(-1, P, P).transpose(1, 0, 2).reshape(P, -1)

    masks = (np.arange(P)[:, None] // CH % HPG == np.arange(HPG)[None, :]).astype(f32)
    groups = (np.arange(P)[:, None] // QUAD == np.arange(GROUPS)[None, :]).astype(f32)
    row_bv = np.repeat(l1["bv"].reshape(HEADS, CH).T, Q_LOW, axis=0)
    vectors = np.concatenate(
        [a["cond_1024"].T, masks, groups, np.eye(P, dtype=f32), columns(l0["b_ada"]), columns(l1["bada"]),
         columns(l0["b_proj"]), columns(l1["bo"]), columns(l0["b_mlp1"]), columns(l1["b1"]),
         columns(l0["b_mlp2"]), columns(l1["b2"]), columns(l1["bq"]), columns(l1["bk"]), row_bv], axis=1)
    w_k, w_q, w_v = np.split(l0["w_qkv"], 3, axis=1)
    weights0 = np.concatenate([l0["w_ada"], w_q, w_k, w_v, l0["w_proj"], l0["w_mlp1"], down(l0["w_mlp2"])], axis=1)
    w_o1 = l1["Wo"].reshape(P // CH, CH, P).transpose(1, 0, 2).reshape(P, P)
    weights1 = np.concatenate([l1["Wada"], l1["Wq"], l1["Wk"], l1["Wv"], w_o1, l1["W1"], down(l1["W2"])], axis=1)
    arrays = {
        "x": np.ascontiguousarray(a["x"].reshape(TILES, P, P).transpose(1, 0, 2).reshape(P, -1)),
        "vectors": np.ascontiguousarray(vectors),
        "weights0": np.ascontiguousarray(weights0),
        "weights1": np.ascontiguousarray(weights1),
    }
    nc = bacc.Bacc("TRN2", target_bir_lowering=False, num_devices=1)
    args = [nc.dram_tensor(f"{name}_dram", v.shape, F32, kind="ExternalInput").ap() for name, v in arrays.items()]
    out = nc.dram_tensor("out_dram", (P, TILES * P), F32, kind="ExternalOutput").ap()
    two_blocks(nc, *args, out)
    r = run_bass_kernel_spmd(nc, [{f"{name}_dram": v for name, v in arrays.items()}], core_ids=[0])
    y = r.results[0]["out_dram"]
    return np.asarray(y).reshape(P, TILES, P).transpose(1, 0, 2).reshape(BATCH, SEQ, P)
```
